# Optimizing a Trainium2 kernel written in Bass

```python
import numpy as np
import jax
import jax.numpy as jnp

def _softmax(x, axis=-1):
    return jax.nn.softmax(x, axis=axis)

def _gelu(x):
    return jax.nn.gelu(x, approximate=True)

def _silu(x):
    return jax.nn.silu(x)

def _sigmoid(x):
    return jax.nn.sigmoid(x)

def _layernorm(x, axis=-1, eps=1e-05):
    m = jnp.mean(x, axis=axis, keepdims=True)
    v = jnp.var(x, axis=axis, keepdims=True)
    return (x - m) / jnp.sqrt(v + eps)

def _scatter_add(tgt, idx, src, axis=0):
    return tgt.at[idx].add(src)

def _segment_sum(src, seg, n):
    return jax.ops.segment_sum(src, seg, n)
kernel_name = 'mk_xattn_seq_d4_seqx_r4_f46daa'

def setup_inputs(seed: int=0):
    np.random.seed(seed)
    _w = jnp.asarray

    def _rec_inputs():
        import jax
        import jax.numpy as jnp
        _rk = jax.random.key(seed)
        x = -0.0001548 + 1 * jax.random.normal(jax.random.fold_in(_rk, 1), (4, 512, 320), jnp.float32)
        _lenS = 512 - jax.random.randint(jax.random.fold_in(_rk, 7), (4,), 0, max(1, 512 // 4) + 1, jnp.int32)
        _lenS2 = 512 - jax.random.randint(jax.random.fold_in(_rk, 8), (4,), 0, max(1, 512 // 4) + 1, jnp.int32)
        _ctx_768P = jax.random.normal(jax.random.fold_in(_rk, 11), (4, 16, 192), jnp.float32)
        _ctx_768c = jax.random.dirichlet(jax.random.fold_in(_rk, 511), 0.3 * jnp.ones((16,), jnp.float32), (4, 512))
        _ctx_768t = jnp.einsum('bsk,bkd->bsd', _ctx_768c, _ctx_768P)
        _ctx_768t = _ctx_768t * jax.lax.rsqrt(jnp.mean(jnp.square(_ctx_768t)) + 1e-12) * 0.953939
        ctx_768 = 0.000651243 + 0.998673 * (_ctx_768t + 0.3 * jax.random.normal(jax.random.fold_in(_rk, 611), (4, 512, 192), jnp.float32))
        return (x, ctx_768)
    x, ctx_768 = _rec_inputs()

    def _L0_xattn_setup():
        import jax, jax.numpy as jnp
        import numpy as np
        DIM, HEADS, DHEAD, CTX_DIM, DFF = (320, 20, 64, 192, 1280)
        EPS = 1e-05
        SCALE = DHEAD ** (-0.5)

        def layer_norm(x, g, b):
            mu = jnp.mean(x, axis=-1, keepdims=True)
            var = jnp.mean(jnp.square(x - mu), axis=-1, keepdims=True)
            return (x - mu) * jax.lax.rsqrt(var + EPS) * g + b

        def cross_attention(x, ctx, wq, wk, wv, wo, bo):
            B, N, _ = x.shape
            M = ctx.shape[1]
            q = jnp.einsum('bne,ef->bnf', x, wq).reshape(B, N, HEADS, DHEAD).transpose(0, 2, 1, 3)
            k = jnp.einsum('bme,ef->bmf', ctx, wk).reshape(B, M, HEADS, DHEAD).transpose(0, 2, 1, 3)
            v = jnp.einsum('bme,ef->bmf', ctx, wv).reshape(B, M, HEADS, DHEAD).transpose(0, 2, 1, 3)
            scores = jnp.einsum('bhnd,bhmd->bhnm', q, k) * SCALE
            attn = jax.nn.softmax(scores, axis=-1)
            out = jnp.einsum('bhnm,bhmd->bhnd', attn, v)
            out = out.transpose(0, 2, 1, 3).reshape(B, N, HEADS * DHEAD)
            return jnp.einsum('bnf,fe->bne', out, wo) + bo

        def geglu_ff(x, w1, b1, w2, b2):
            h = jnp.einsum('bne,ef->bnf', x, w1) + b1
            a, gate = (h[..., :DFF], h[..., DFF:])
            h = a * jax.nn.gelu(gate)
            return jnp.einsum('bnf,fe->bne', h, w2) + b2

        def block_forward(x, context, g1, be1, wq1, wk1, wv1, wo1, bo1, g2, be2, wq2, wk2, wv2, wo2, bo2, g3, be3, w_ff1, b_ff1, w_ff2, b_ff2):
            x = cross_attention(layer_norm(x, g1, be1), layer_norm(x, g1, be1), wq1, wk1, wv1, wo1, bo1) + x
            x = cross_attention(layer_norm(x, g2, be2), context, wq2, wk2, wv2, wo2, bo2) + x
            return geglu_ff(layer_norm(x, g3, be3), w_ff1, b_ff1, w_ff2, b_ff2) + x
        key = jax.random.key(seed)
        ks = jax.random.split(key, 20)
        s = 0.02
        inner = HEADS * DHEAD
        return {'x': jax.random.normal(ks[0], (4, 256, DIM), jnp.float32), 'context': jax.random.normal(ks[1], (4, 77, CTX_DIM), jnp.float32), 'g1': jnp.ones((DIM,), jnp.float32), 'be1': jnp.zeros((DIM,), jnp.float32), 'wq1': jax.random.normal(ks[2], (DIM, inner), jnp.float32) * s, 'wk1': jax.random.normal(ks[3], (DIM, inner), jnp.float32) * s, 'wv1': jax.random.normal(ks[4], (DIM, inner), jnp.float32) * s, 'wo1': jax.random.normal(ks[5], (inner, DIM), jnp.float32) * s, 'bo1': jnp.zeros((DIM,), jnp.float32), 'g2': jnp.ones((DIM,), jnp.float32), 'be2': jnp.zeros((DIM,), jnp.float32), 'wq2': jax.random.normal(ks[6], (DIM, inner), jnp.float32) * s, 'wk2': jax.random.normal(ks[7], (CTX_DIM, inner), jnp.float32) * s, 'wv2': jax.random.normal(ks[8], (CTX_DIM, inner), jnp.float32) * s, 'wo2': jax.random.normal(ks[9], (inner, DIM), jnp.float32) * s, 'bo2': jnp.zeros((DIM,), jnp.float32), 'g3': jnp.ones((DIM,), jnp.float32), 'be3': jnp.zeros((DIM,), jnp.float32), 'w_ff1': jax.random.normal(ks[10], (DIM, 2 * DFF), jnp.float32) * s, 'b_ff1': jnp.zeros((2 * DFF,), jnp.float32), 'w_ff2': jax.random.normal(ks[11], (DFF, DIM), jnp.float32) * s, 'b_ff2': jnp.zeros((DIM,), jnp.float32)}
    _L0_xattn_all = _L0_xattn_setup()
    _L0_xattn_in = {k: v for k, v in _L0_xattn_all.items() if k in ('g1', 'be1', 'wq1', 'wk1', 'wv1', 'wo1', 'bo1', 'g2', 'be2', 'wq2', 'wk2', 'wv2', 'wo2', 'bo2', 'g3', 'be3', 'w_ff1', 'b_ff1', 'w_ff2', 'b_ff2')}
    del _L0_xattn_all

    def _L1_xattn_setup():
        import jax, jax.numpy as jnp
        import numpy as np
        D = 320
        H = 20
        DH = D // H
        CTX = 192
        FF_IN = 4 * D
        EPS = 1e-05

        def _ln(x, g, b):
            m = jnp.mean(x, axis=-1, keepdims=True)
            v = jnp.mean(jnp.square(x - m), axis=-1, keepdims=True)
            return (x - m) * jax.lax.rsqrt(v + EPS) * g + b

        def _attn(x, ctx, wq, wk, wv, wo, bo, heads):
            b, n, _ = x.shape
            j = ctx.shape[1]
            dh = wq.shape[1] // heads
            scale = dh ** (-0.5)
            q = (x @ wq).reshape(b, n, heads, dh).transpose(0, 2, 1, 3)
            k = (ctx @ wk).reshape(b, j, heads, dh).transpose(0, 2, 1, 3)
            v = (ctx @ wv).reshape(b, j, heads, dh).transpose(0, 2, 1, 3)
            sim = jnp.einsum('bhid,bhjd->bhij', q, k) * scale
            a = jax.nn.softmax(sim, axis=-1)
            out = jnp.einsum('bhij,bhjd->bhid', a, v)
            out = out.transpose(0, 2, 1, 3).reshape(b, n, heads * dh)
            return out @ wo + bo
        key = jax.random.key(seed)
        ks = jax.random.split(key, 24)
        r = lambda k, shp, s: jax.random.normal(k, shp, dtype=jnp.float32) * s
        d = {'x': r(ks[0], (8, 256, D), 1.0), 'context': r(ks[1], (8, 77, CTX), 1.0), 'heads': H, 'n1_g': jnp.ones((D,), jnp.float32), 'n1_b': jnp.zeros((D,), jnp.float32), 'q1': r(ks[2], (D, D), D ** (-0.5)), 'k1': r(ks[3], (D, D), D ** (-0.5)), 'v1': r(ks[4], (D, D), D ** (-0.5)), 'o1_w': r(ks[5], (D, D), D ** (-0.5)), 'o1_b': jnp.zeros((D,), jnp.float32), 'n2_g': jnp.ones((D,), jnp.float32), 'n2_b': jnp.zeros((D,), jnp.float32), 'q2': r(ks[6], (D, D), D ** (-0.5)), 'k2': r(ks[7], (CTX, D), CTX ** (-0.5)), 'v2': r(ks[8], (CTX, D), CTX ** (-0.5)), 'o2_w': r(ks[9], (D, D), D ** (-0.5)), 'o2_b': jnp.zeros((D,), jnp.float32), 'n3_g': jnp.ones((D,), jnp.float32), 'n3_b': jnp.zeros((D,), jnp.float32), 'ff_w1': r(ks[10], (D, 2 * FF_IN), D ** (-0.5)), 'ff_b1': jnp.zeros((2 * FF_IN,), jnp.float32), 'ff_w2': r(ks[11], (FF_IN, D), FF_IN ** (-0.5)), 'ff_b2': jnp.zeros((D,), jnp.float32)}
        return d
    _L1_xattn_all = _L1_xattn_setup()
    _L1_xattn_in = {k: v for k, v in _L1_xattn_all.items() if k in ('n1_g', 'n1_b', 'q1', 'k1', 'v1', 'o1_w', 'o1_b', 'n2_g', 'n2_b', 'q2', 'k2', 'v2', 'o2_w', 'o2_b', 'n3_g', 'n3_b', 'ff_w1', 'ff_b1', 'ff_w2', 'ff_b2')}
    del _L1_xattn_all

    def _L2_xattn_setup():
        import jax, jax.numpy as jnp
        import numpy as np
        B, S, D = (32, 256, 320)
        CROSS = 192
        HEADS = 20
        HD = D // HEADS
        N_AOE, N_IMG = (16, 16)
        SCALE = 1.0 / float(np.sqrt(HD))

        def _split_heads(x):
            b, n, _ = x.shape
            return x.reshape(b, n, HEADS, HD).transpose(0, 2, 1, 3)

        def _attend(q, k, v):
            scores = jnp.einsum('bhsd,bhkd->bhsk', q, k) * SCALE
            probs = jax.nn.softmax(scores, axis=-1)
            return jnp.einsum('bhsk,bhkd->bhsd', probs, v)
        key = jax.random.key(seed)
        ks = jax.random.split(key, 10)
        g = lambda k, shape, sc=0.02: jax.random.normal(k, shape, jnp.float32) * sc
        return {'hidden_states': jax.random.normal(ks[0], (B, S, D), jnp.float32), 'encoder_hidden_states': jax.random.normal(ks[1], (B, N_AOE + N_IMG + 16, CROSS), jnp.float32), 'w_q': g(ks[2], (D, D)), 'w_k': g(ks[3], (D, CROSS)), 'w_v': g(ks[4], (D, CROSS)), 'w_k_dis': g(ks[5], (D, CROSS)), 'w_v_dis': g(ks[6], (D, CROSS)), 'w_gate': g(ks[7], (1, CROSS)), 'b_gate': jnp.zeros((1,), jnp.float32), 'anat_gate_logit': jnp.float32(0.0), 'dis_gate_logit': jnp.float32(0.0), 'w_out': g(ks[8], (D, D)), 'b_out': jnp.zeros((D,), jnp.float32)}
    _L2_xattn_all = _L2_xattn_setup()
    _L2_xattn_in = {k: v for k, v in _L2_xattn_all.items() if k in ('w_q', 'w_k', 'w_v', 'w_k_dis', 'w_v_dis', 'w_gate', 'b_gate', 'anat_gate_logit', 'dis_gate_logit', 'w_out', 'b_out')}
    del _L2_xattn_all

    def _L3_xattn_setup():
        import jax, jax.numpy as jnp
        import numpy as np
        HEADS = 20
        NUM_AOE = 16
        NUM_IP = 16
        key = jax.random.key(seed)
        ks = jax.random.split(key, 7)
        B, Sq, H = (8, 1024, 320)
        Skv, C = (109, 192)
        scale = 0.02
        return {'hidden_states': jax.random.normal(ks[0], (B, Sq, H), jnp.float32), 'encoder_hidden_states': jax.random.normal(ks[1], (B, Skv, C), jnp.float32), 'Wq': jax.random.normal(ks[2], (H, H), jnp.float32) * scale, 'Wk': jax.random.normal(ks[3], (C, H), jnp.float32) * scale, 'Wv': jax.random.normal(ks[4], (C, H), jnp.float32) * scale, 'Wo': jax.random.normal(ks[5], (H, H), jnp.float32) * scale, 'bo': jnp.zeros((H,), jnp.float32)}
    _L3_xattn_all = _L3_xattn_setup()
    _L3_xattn_in = {k: v for k, v in _L3_xattn_all.items() if k in ('Wq', 'Wk', 'Wv', 'Wo', 'bo')}
    del _L3_xattn_all
    return {'x': x, 'ctx_768': ctx_768, 'L0_xattn_g1': _L0_xattn_in['g1'], 'L0_xattn_be1': _L0_xattn_in['be1'], 'L0_xattn_wq1': _L0_xattn_in['wq1'], 'L0_xattn_wk1': _L0_xattn_in['wk1'], 'L0_xattn_wv1': _L0_xattn_in['wv1'], 'L0_xattn_wo1': _L0_xattn_in['wo1'], 'L0_xattn_bo1': _L0_xattn_in['bo1'], 'L0_xattn_g2': _L0_xattn_in['g2'], 'L0_xattn_be2': _L0_xattn_in['be2'], 'L0_xattn_wq2': _L0_xattn_in['wq2'], 'L0_xattn_wk2': _L0_xattn_in['wk2'], 'L0_xattn_wv2': _L0_xattn_in['wv2'], 'L0_xattn_wo2': _L0_xattn_in['wo2'], 'L0_xattn_bo2': _L0_xattn_in['bo2'], 'L0_xattn_g3': _L0_xattn_in['g3'], 'L0_xattn_be3': _L0_xattn_in['be3'], 'L0_xattn_w_ff1': _L0_xattn_in['w_ff1'], 'L0_xattn_b_ff1': _L0_xattn_in['b_ff1'], 'L0_xattn_w_ff2': _L0_xattn_in['w_ff2'], 'L0_xattn_b_ff2': _L0_xattn_in['b_ff2'], 'L1_xattn_n1_g': _L1_xattn_in['n1_g'], 'L1_xattn_n1_b': _L1_xattn_in['n1_b'], 'L1_xattn_q1': _L1_xattn_in['q1'], 'L1_xattn_k1': _L1_xattn_in['k1'], 'L1_xattn_v1': _L1_xattn_in['v1'], 'L1_xattn_o1_w': _L1_xattn_in['o1_w'], 'L1_xattn_o1_b': _L1_xattn_in['o1_b'], 'L1_xattn_n2_g': _L1_xattn_in['n2_g'], 'L1_xattn_n2_b': _L1_xattn_in['n2_b'], 'L1_xattn_q2': _L1_xattn_in['q2'], 'L1_xattn_k2': _L1_xattn_in['k2'], 'L1_xattn_v2': _L1_xattn_in['v2'], 'L1_xattn_o2_w': _L1_xattn_in['o2_w'], 'L1_xattn_o2_b': _L1_xattn_in['o2_b'], 'L1_xattn_n3_g': _L1_xattn_in['n3_g'], 'L1_xattn_n3_b': _L1_xattn_in['n3_b'], 'L1_xattn_ff_w1': _L1_xattn_in['ff_w1'], 'L1_xattn_ff_b1': _L1_xattn_in['ff_b1'], 'L1_xattn_ff_w2': _L1_xattn_in['ff_w2'], 'L1_xattn_ff_b2': _L1_xattn_in['ff_b2'], 'L2_xattn_w_q': _L2_xattn_in['w_q'], 'L2_xattn_w_k': _L2_xattn_in['w_k'], 'L2_xattn_w_v': _L2_xattn_in['w_v'], 'L2_xattn_w_k_dis': _L2_xattn_in['w_k_dis'], 'L2_xattn_w_v_dis': _L2_xattn_in['w_v_dis'], 'L2_xattn_w_gate': _L2_xattn_in['w_gate'], 'L2_xattn_b_gate': _L2_xattn_in['b_gate'], 'L2_xattn_anat_gate_logit': _L2_xattn_in['anat_gate_logit'], 'L2_xattn_dis_gate_logit': _L2_xattn_in['dis_gate_logit'], 'L2_xattn_w_out': _L2_xattn_in['w_out'], 'L2_xattn_b_out': _L2_xattn_in['b_out'], 'L3_xattn_Wq': _L3_xattn_in['Wq'], 'L3_xattn_Wk': _L3_xattn_in['Wk'], 'L3_xattn_Wv': _L3_xattn_in['Wv'], 'L3_xattn_Wo': _L3_xattn_in['Wo'], 'L3_xattn_bo': _L3_xattn_in['bo']}

def reference(x, ctx_768, L0_xattn_g1, L0_xattn_be1, L0_xattn_wq1, L0_xattn_wk1, L0_xattn_wv1, L0_xattn_wo1, L0_xattn_bo1, L0_xattn_g2, L0_xattn_be2, L0_xattn_wq2, L0_xattn_wk2, L0_xattn_wv2, L0_xattn_wo2, L0_xattn_bo2, L0_xattn_g3, L0_xattn_be3, L0_xattn_w_ff1, L0_xattn_b_ff1, L0_xattn_w_ff2, L0_xattn_b_ff2, L1_xattn_n1_g, L1_xattn_n1_b, L1_xattn_q1, L1_xattn_k1, L1_xattn_v1, L1_xattn_o1_w, L1_xattn_o1_b, L1_xattn_n2_g, L1_xattn_n2_b, L1_xattn_q2, L1_xattn_k2, L1_xattn_v2, L1_xattn_o2_w, L1_xattn_o2_b, L1_xattn_n3_g, L1_xattn_n3_b, L1_xattn_ff_w1, L1_xattn_ff_b1, L1_xattn_ff_w2, L1_xattn_ff_b2, L2_xattn_w_q, L2_xattn_w_k, L2_xattn_w_v, L2_xattn_w_k_dis, L2_xattn_w_v_dis, L2_xattn_w_gate, L2_xattn_b_gate, L2_xattn_anat_gate_logit, L2_xattn_dis_gate_logit, L2_xattn_w_out, L2_xattn_b_out, L3_xattn_Wq, L3_xattn_Wk, L3_xattn_Wv, L3_xattn_Wo, L3_xattn_bo):
    import jax
    import jax.numpy as jnp

    def _L0_xattn_ref(x, context, g1, be1, wq1, wk1, wv1, wo1, bo1, g2, be2, wq2, wk2, wv2, wo2, bo2, g3, be3, w_ff1, b_ff1, w_ff2, b_ff2):
        import jax, jax.numpy as jnp
        import numpy as np
        DIM, HEADS, DHEAD, CTX_DIM, DFF = (320, 20, 64, 192, 1280)
        EPS = 1e-05
        SCALE = DHEAD ** (-0.5)

        def layer_norm(x, g, b):
            mu = jnp.mean(x, axis=-1, keepdims=True)
            var = jnp.mean(jnp.square(x - mu), axis=-1, keepdims=True)
            return (x - mu) * jax.lax.rsqrt(var + EPS) * g + b

        def cross_attention(x, ctx, wq, wk, wv, wo, bo):
            B, N, _ = x.shape
            M = ctx.shape[1]
            q = jnp.einsum('bne,ef->bnf', x, wq).reshape(B, N, HEADS, DHEAD).transpose(0, 2, 1, 3)
            k = jnp.einsum('bme,ef->bmf', ctx, wk).reshape(B, M, HEADS, DHEAD).transpose(0, 2, 1, 3)
            v = jnp.einsum('bme,ef->bmf', ctx, wv).reshape(B, M, HEADS, DHEAD).transpose(0, 2, 1, 3)
            scores = jnp.einsum('bhnd,bhmd->bhnm', q, k) * SCALE
            attn = jax.nn.softmax(scores, axis=-1)
            out = jnp.einsum('bhnm,bhmd->bhnd', attn, v)
            out = out.transpose(0, 2, 1, 3).reshape(B, N, HEADS * DHEAD)
            return jnp.einsum('bnf,fe->bne', out, wo) + bo

        def geglu_ff(x, w1, b1, w2, b2):
            h = jnp.einsum('bne,ef->bnf', x, w1) + b1
            a, gate = (h[..., :DFF], h[..., DFF:])
            h = a * jax.nn.gelu(gate)
            return jnp.einsum('bnf,fe->bne', h, w2) + b2

        def block_forward(x, context, g1, be1, wq1, wk1, wv1, wo1, bo1, g2, be2, wq2, wk2, wv2, wo2, bo2, g3, be3, w_ff1, b_ff1, w_ff2, b_ff2):
            x = cross_attention(layer_norm(x, g1, be1), layer_norm(x, g1, be1), wq1, wk1, wv1, wo1, bo1) + x
            x = cross_attention(layer_norm(x, g2, be2), context, wq2, wk2, wv2, wo2, bo2) + x
            return geglu_ff(layer_norm(x, g3, be3), w_ff1, b_ff1, w_ff2, b_ff2) + x
        return block_forward(x, context, g1, be1, wq1, wk1, wv1, wo1, bo1, g2, be2, wq2, wk2, wv2, wo2, bo2, g3, be3, w_ff1, b_ff1, w_ff2, b_ff2)

    def _L1_xattn_ref(x, context, heads, n1_g, n1_b, q1, k1, v1, o1_w, o1_b, n2_g, n2_b, q2, k2, v2, o2_w, o2_b, n3_g, n3_b, ff_w1, ff_b1, ff_w2, ff_b2):
        import jax, jax.numpy as jnp
        import numpy as np
        D = 320
        H = 20
        DH = D // H
        CTX = 192
        FF_IN = 4 * D
        EPS = 1e-05

        def _ln(x, g, b):
            m = jnp.mean(x, axis=-1, keepdims=True)
            v = jnp.mean(jnp.square(x - m), axis=-1, keepdims=True)
            return (x - m) * jax.lax.rsqrt(v + EPS) * g + b

        def _attn(x, ctx, wq, wk, wv, wo, bo, heads):
            b, n, _ = x.shape
            j = ctx.shape[1]
            dh = wq.shape[1] // heads
            scale = dh ** (-0.5)
            q = (x @ wq).reshape(b, n, heads, dh).transpose(0, 2, 1, 3)
            k = (ctx @ wk).reshape(b, j, heads, dh).transpose(0, 2, 1, 3)
            v = (ctx @ wv).reshape(b, j, heads, dh).transpose(0, 2, 1, 3)
            sim = jnp.einsum('bhid,bhjd->bhij', q, k) * scale
            a = jax.nn.softmax(sim, axis=-1)
            out = jnp.einsum('bhij,bhjd->bhid', a, v)
            out = out.transpose(0, 2, 1, 3).reshape(b, n, heads * dh)
            return out @ wo + bo
        h1 = _ln(x, n1_g, n1_b)
        x = _attn(h1, h1, q1, k1, v1, o1_w, o1_b, heads) + x
        h2 = _ln(x, n2_g, n2_b)
        x = _attn(h2, context, q2, k2, v2, o2_w, o2_b, heads) + x
        h3 = _ln(x, n3_g, n3_b)
        proj = h3 @ ff_w1 + ff_b1
        a, g = jnp.split(proj, 2, axis=-1)
        ff = a * jax.nn.gelu(g, approximate=False) @ ff_w2 + ff_b2
        return ff + x

    def _L2_xattn_ref(hidden_states, encoder_hidden_states, w_q, w_k, w_v, w_k_dis, w_v_dis, w_gate, b_gate, anat_gate_logit, dis_gate_logit, w_out, b_out):
        import jax, jax.numpy as jnp
        import numpy as np
        B, S, D = (32, 256, 320)
        CROSS = 192
        HEADS = 20
        HD = D // HEADS
        N_AOE, N_IMG = (16, 16)
        SCALE = 1.0 / float(np.sqrt(HD))

        def _split_heads(x):
            b, n, _ = x.shape
            return x.reshape(b, n, HEADS, HD).transpose(0, 2, 1, 3)

        def _attend(q, k, v):
            scores = jnp.einsum('bhsd,bhkd->bhsk', q, k) * SCALE
            probs = jax.nn.softmax(scores, axis=-1)
            return jnp.einsum('bhsk,bhkd->bhsd', probs, v)
        residual = hidden_states
        b = hidden_states.shape[0]
        dis_tokens = encoder_hidden_states[:, :N_AOE, :]
        anat_tokens = encoder_hidden_states[:, N_AOE:N_AOE + N_IMG, :]
        query = _split_heads(hidden_states @ w_q.T)
        k_anat = _split_heads(anat_tokens @ w_k.T)
        v_anat = _split_heads(anat_tokens @ w_v.T)
        k_dis = _split_heads(dis_tokens @ w_k_dis.T)
        v_dis = _split_heads(dis_tokens @ w_v_dis.T)
        z_anat = _attend(query, k_anat, v_anat)
        z_dis = _attend(query, k_dis, v_dis)
        severity = dis_tokens.mean(axis=1)
        shift = (severity @ w_gate.T + b_gate).reshape(b, 1, 1, 1)
        anat_gate = jax.nn.sigmoid(anat_gate_logit - shift)
        dis_gate = jax.nn.sigmoid(dis_gate_logit + shift)
        z_final = anat_gate * z_anat + dis_gate * z_dis
        out = z_final.transpose(0, 2, 1, 3).reshape(b, -1, D)
        out = out @ w_out.T + b_out
        out = out + residual
        return out

    def _L3_xattn_ref(hidden_states, encoder_hidden_states, Wq, Wk, Wv, Wo, bo):
        import jax, jax.numpy as jnp
        import numpy as np
        HEADS = 20
        NUM_AOE = 16
        NUM_IP = 16
        B, Sq, H = hidden_states.shape
        Skv = encoder_hidden_states.shape[1]
        head_dim = H // HEADS
        residual = hidden_states
        q = (hidden_states @ Wq).reshape(B, Sq, HEADS, head_dim).transpose(0, 2, 1, 3)
        k = (encoder_hidden_states @ Wk).reshape(B, Skv, HEADS, head_dim).transpose(0, 2, 1, 3)
        v = (encoder_hidden_states @ Wv).reshape(B, Skv, HEADS, head_dim).transpose(0, 2, 1, 3)
        scores = jnp.einsum('bhqd,bhkd->bhqk', q, k) / jnp.sqrt(jnp.asarray(head_dim, q.dtype))
        probs = jax.nn.softmax(scores, axis=-1)
        scale_aoe = jnp.asarray(1.0, probs.dtype)
        scale_ip = jnp.asarray(1.0, probs.dtype)
        idx = jnp.arange(Skv)
        scale_vector = jnp.where(idx < NUM_AOE, scale_aoe, 1.0)
        scale_vector = jnp.where(idx >= Skv - NUM_IP, scale_vector * scale_ip, scale_vector)
        probs = probs * scale_vector
        probs = probs / probs.sum(axis=-1, keepdims=True)
        out = jnp.einsum('bhqk,bhkd->bhqd', probs, v)
        out = out.transpose(0, 2, 1, 3).reshape(B, Sq, H)
        out = out @ Wo + bo
        return out + residual
    x = _L0_xattn_ref(x, ctx_768, L0_xattn_g1, L0_xattn_be1, L0_xattn_wq1, L0_xattn_wk1, L0_xattn_wv1, L0_xattn_wo1, L0_xattn_bo1, L0_xattn_g2, L0_xattn_be2, L0_xattn_wq2, L0_xattn_wk2, L0_xattn_wv2, L0_xattn_wo2, L0_xattn_bo2, L0_xattn_g3, L0_xattn_be3, L0_xattn_w_ff1, L0_xattn_b_ff1, L0_xattn_w_ff2, L0_xattn_b_ff2)
    x = _L1_xattn_ref(x, ctx_768, 20, L1_xattn_n1_g, L1_xattn_n1_b, L1_xattn_q1, L1_xattn_k1, L1_xattn_v1, L1_xattn_o1_w, L1_xattn_o1_b, L1_xattn_n2_g, L1_xattn_n2_b, L1_xattn_q2, L1_xattn_k2, L1_xattn_v2, L1_xattn_o2_w, L1_xattn_o2_b, L1_xattn_n3_g, L1_xattn_n3_b, L1_xattn_ff_w1, L1_xattn_ff_b1, L1_xattn_ff_w2, L1_xattn_ff_b2)
    x = _L2_xattn_ref(x, ctx_768, L2_xattn_w_q, L2_xattn_w_k, L2_xattn_w_v, L2_xattn_w_k_dis, L2_xattn_w_v_dis, L2_xattn_w_gate, L2_xattn_b_gate, L2_xattn_anat_gate_logit, L2_xattn_dis_gate_logit, L2_xattn_w_out, L2_xattn_b_out)
    x = _L3_xattn_ref(x, ctx_768, L3_xattn_Wq, L3_xattn_Wk, L3_xattn_Wv, L3_xattn_Wo, L3_xattn_bo)
    return x

_drawn_inputs = setup_inputs


def setup_inputs(seed=0):
    import zlib

    import numpy as np

    out = dict(_drawn_inputs(seed))
    spreads = {'L0_xattn_g1': (1.0, 0.6),
     'L0_xattn_be1': (0.0, 0.1),
     'L0_xattn_bo1': (0.0, 0.1),
     'L0_xattn_g2': (1.0, 0.6),
     'L0_xattn_be2': (0.0, 0.8),
     'L0_xattn_bo2': (0.0, 0.1),
     'L0_xattn_g3': (1.0, 0.6),
     'L0_xattn_be3': (0.0, 0.8),
     'L0_xattn_b_ff1': (0.0, 0.375),
     'L0_xattn_b_ff2': (0.0, 0.1),
     'L1_xattn_n1_g': (1.0, 0.2),
     'L1_xattn_n1_b': (0.0, 0.1),
     'L1_xattn_o1_b': (0.0, 0.1),
     'L1_xattn_n2_g': (1.0, 0.2),
     'L1_xattn_n2_b': (0.0, 0.403),
     'L1_xattn_o2_b': (0.0, 0.1),
     'L1_xattn_n3_g': (1.0, 0.2),
     'L1_xattn_n3_b': (0.0, 0.1),
     'L1_xattn_ff_b1': (0.0, 0.1),
     'L1_xattn_ff_b2': (0.0, 0.1),
     'L2_xattn_b_out': (0.0, 0.1),
     'L3_xattn_bo': (0.0, 0.1)}
    factors = {'L0_xattn_wq1': 8.0,
     'L0_xattn_wk1': 8.0,
     'L0_xattn_wq2': 8.0,
     'L0_xattn_wk2': 8.0,
     'L2_xattn_w_q': 8.0,
     'L2_xattn_w_k': 8.0,
     'L2_xattn_w_v': 3.098,
     'L2_xattn_w_k_dis': 8.0,
     'L2_xattn_w_gate': 8.0,
     'L3_xattn_Wq': 8.0,
     'L3_xattn_Wk': 8.0}
    for name, (base, spread) in spreads.items():
        noise = np.random.default_rng([zlib.crc32(name.encode()), seed]).standard_normal(out[name].shape)
        drawn = base * np.exp(spread * noise) if base else spread * noise
        out[name] = jnp.asarray(drawn.astype(out[name].dtype))
    for name, factor in factors.items():
        out[name] = (out[name] * factor).astype(out[name].dtype)
    return out
```

```python
from contextlib import ExitStack

import concourse.bass as bass
from concourse import mybir

F32 = mybir.dt.float32
BF16 = mybir.dt.bfloat16
ALU = mybir.AluOpType
ACT = mybir.ActivationFunctionType
AX = mybir.AxisListType

P = 128
B = 4
N = 512
TB = N // P
D = 320
CD = 192
HEADS = 20
DFF = 1280
EPS = 1e-5
CH = [(0, 128), (128, 128), (256, 64)]
CCH = [(0, 128), (128, 64)]
ITERS = 2
PAIRS = 5
HPI = 2 * PAIRS
X_IN = 16
NTOK = 16
Q_PARTS = "hmhlhm"
K_PARTS = "hhmhlm"


def after(n, per, k):
    return n * per + max(k, 0)


SEEDED = ("q_ps", "k_ps", "q_evac", "k_evac", "rows", "max", "nm_ps", "nm_hi", "nm_lo", "st", "exp", "av", "on", "rec")


def seeded(n, per, k):
    return after(n, per, k) + 1


class Memory:

    def __init__(self, nc, ctx):
        def sb(name, shape, dt=F32):
            return ctx.enter_context(nc.sbuf_tensor(name, shape, dt))

        self.x = sb("x_res", [P, B * TB, D])
        self.weights = sb("weights", [P, 3 * 2 * DFF + 10 * D])
        self.heads = sb("heads", [P, 10240])
        self.values = sb("values", [P, TB * HEADS * 65])
        self.mixed = sb("mixed", [P, 10 * N])
        self.probs = sb("probs", [P, 2, TB, N])
        self.xn = sb("xn", [P, TB, D])
        self.ctx_in = sb("ctx_in", [P, TB, CD])
        self.hT = sb("hT", [P, 3, N])
        self.cT = sb("cT", [P, 2, N])
        self.ident = sb("ident", [P, P])
        self.sel = sb("sel", [P, P], BF16)
        self.nmT = sb("nmT", [P, 2, N], BF16)
        self.negm = sb("negm", [P, 2, TB, 2])
        self.rec = sb("rec", [P, 2, TB])
        self.stats = sb("stats", [P, TB, 6])
        self.mv = sb("mv", [P, TB, 2])
        self.rstd = sb("rstd", [P, TB])
        self.vare = sb("vare", [P, TB])
        self.mhalf = sb("mhalf", [P, TB])
        self.g_col = sb("g_col", [P, 3])
        self.b_col = sb("b_col", [P, 3])
        self.b1_col = sb("b1_col", [P, 2 * DFF // P])
        self.bo_row = sb("bo_row", [P, D])
        self.ysum = sb("ysum", [P, 2, D])
        self.small = sb("small", [P, 64])
        self.bank = [ctx.enter_context(nc.psum_tensor(f"bank{i}", [P, 512], F32)) for i in range(8)]
        self.PJ = self.bank[0:2]
        self.SM = self.bank[2:4]
        self.ST = self.bank[4:6]
        self.OB = self.bank[6]
        self.TR = self.bank[7]


class Stage:

    def __init__(self, nc, ctx, name, index, like=None, **kw):
        self.name, self.index, self.nc, self.ctx = name, index, nc, ctx
        self.sems = like.sems if like else {}
        self.first = like.first + B if like else 0
        self.kind = kw.pop("kind")
        self.prm = kw
        self.tag = name
        self.w_in = ctx.enter_context(nc.semaphore(f"{name}_w_in"))

    def sem(self, what):
        if what not in self.sems:
            self.sems[what] = self.ctx.enter_context(self.nc.semaphore(f"{self.name}_{what}"))
        return self.sems[what]


def program(nc, io):
    with ExitStack() as ctx:
        M = Memory(nc, ctx)
        x_done = ctx.enter_context(nc.semaphore("x_done"))
        consts = ctx.enter_context(nc.semaphore("consts"))
        consts0 = ctx.enter_context(nc.semaphore("consts0"))
        x_out = ctx.enter_context(nc.semaphore("x_out"))

        def att(name, i, big, ln, cross, **kw):
            return Stage(nc, ctx, name, i, kind="att", big=big, ln=ln, cross=cross, dh=64 if big else 16, **kw)

        ff0 = Stage(nc, ctx, "s2", 2, kind="ff", ln=True, cross=False, gelu=ACT.Gelu_apprx_tanh, **io["L0f"])
        wide = att("s0", 0, True, True, False, **io["L0a"])
        narrow = att("s3", 3, False, True, False, **io["L1a"])
        narrow2 = att("s4", 4, False, True, True, like=narrow, **io["L1b"])
        stages = [
            wide,
            att("s1", 1, True, True, True, like=wide, **io["L0b"]),
            ff0,
            narrow,
            narrow2,
            Stage(nc, ctx, "s5", 5, like=ff0, kind="ff", ln=True, cross=False, gelu=ACT.Gelu, **io["L1f"]),
            Stage(nc, ctx, "s6", 6, kind="gated", ln=False, cross=True, dh=16, **io["L2"]),
            att("s7", 7, False, False, True, like=narrow2, **io["L3"]),
        ]
        NX = B * TB

        def hold(eng, sem, value):
            eng.wait_ge(sem, value)
            eng.nop(nofuse=True)

        def start(eng, s, b):
            hold(eng, x_done, after(b, TB, (s.index * B - s.first) * TB + X_IN))

        def views(s):
            v = {}
            p = s.prm
            if s.kind == "ff":
                v["w1"] = M.weights[:, 0:3 * 2 * DFF].rearrange("p (c f) -> p c f", c=3)
                v["wo"] = M.weights[:, 3 * 2 * DFF:3 * 2 * DFF + 10 * D].rearrange("p (c f) -> p c f", c=10)
                v["OT"] = M.mixed[:, :].rearrange("p (c n) -> p c n", c=10)
                v["gate"] = M.probs[:, 0, :, :]
                return v
            if s.kind == "att" and p["big"]:
                nk = 2 if p["cross"] else 3
                v["wv"] = M.weights[:, 0:nk * 1280].rearrange("p (c f) -> p c f", c=nk)
                v["wo"] = M.weights[:, 3 * 1280:3 * 1280 + 10 * D].rearrange("p (c f) -> p c f", c=10)
                v["On"] = M.heads[:, 0:5120].rearrange("p (t f) -> p t f", t=TB)
                v["QT"] = M.heads[:, 5120:6144].rearrange("p (s n) -> p s n", s=2)
                v["KT"] = M.heads[:, 6144:7168].rearrange("p (s n) -> p s n", s=2)
                v["QB"] = M.heads[:, 7168:7680].bitcast(BF16).rearrange("p (s n) -> p s n", s=2)
                v["KB"] = M.heads[:, 7680:8192].bitcast(BF16).rearrange("p (s n) -> p s n", s=2)
                v["wqk"] = M.heads[:, 8192:8192 + 2 * (3 + nk) * P].rearrange("p (s c f) -> p s c f", s=2, c=3 + nk)
                v["V"] = M.values[:, :].rearrange("p (t h d) -> p t h d", t=TB, h=HEADS)
                v["OT"] = M.mixed[:, :].rearrange("p (c n) -> p c n", c=10)
                return v
            nk = 2 if p["cross"] else 3
            v["wo"] = M.weights[:, 3 * 1280:3 * 1280 + 3 * D].rearrange("p (c f) -> p c f", c=3)
            v["OT"] = M.mixed[:, 0:1536].rearrange("p (c n) -> p c n", c=3)
            v["On"] = M.mixed[:, 1536:2816].rearrange("p (t f) -> p t f", t=TB)
            if s.kind == "gated":
                return v
            v["wv"] = M.weights[:, 0:nk * D].rearrange("p (c f) -> p c f", c=nk)
            v["wq"] = M.weights[:, 960:1920].rearrange("p (c f) -> p c f", c=3)
            v["wk"] = M.weights[:, 1920:1920 + nk * D].rearrange("p (c f) -> p c f", c=nk)
            v["QS"] = M.heads[:, 0:5120].bitcast(BF16).rearrange("p (h n) -> p h n", h=HEADS)
            v["KS"] = M.heads[:, 5120:10240].bitcast(BF16).rearrange("p (h n) -> p h n", h=HEADS)
            nv = TB * HEADS * 17
            v["V"] = M.values[:, 0:nv].rearrange("p (t h d) -> p t h d", t=TB, h=HEADS)
            v["rest"] = M.values[:, nv:nv + 1024].rearrange("p (s n) -> p s n", s=2)
            v["parts"] = M.values[:, nv + 1024:nv + 2560].bitcast(BF16).rearrange("p (s k n) -> p s k n", s=2, k=3)
            return v

        V = {s.name: views(s) for s in stages}

        def kv_chunks(s):
            return CCH if s.prm["cross"] else CH

        def out_chunks(s):
            return [(P * c, P) for c in range(10)] if s.kind == "ff" or s.prm.get("big") else CH

        def load_weights(sp, s):
            start(sp, s, s.first)
            p, v, n = s.prm, V[s.name], 0
            w_in = s.w_in

            def load(dst, src):
                nonlocal n
                sp.dma_start(dst, src).then_inc(w_in, 16)
                n += 1

            def load_chunks(dst, src, chunks):
                full = len([1 for _, w in chunks if w == P])
                load(dst[:, 0:full, :], src[0:full * P, :].rearrange("(c p) f -> p c f", p=P))
                if full < len(chunks):
                    a, w = chunks[full]
                    load(dst[0:w, full, :], src[a:a + w, :])

            if p["ln"]:
                load(M.g_col[:, :], p["g"])
                load(M.b_col[:, :], p["be"])
            load(M.bo_row[:, :], p["bo"].rearrange("(a d) -> a d", a=1).broadcast_to([P, D]))
            load_chunks(v["wo"], p["wo"], out_chunks(s))
            if s.kind == "att":
                load_chunks(v["wv"], p["wv"], kv_chunks(s))
                if not p["big"]:
                    load_chunks(v["wq"], p["wq"], CH)
                    load_chunks(v["wk"], p["wk"], kv_chunks(s))
            elif s.kind == "ff":
                load_chunks(v["w1"], p["w1"], CH)
                load(M.b1_col[:, :], p["b1"])
            else:
                load_chunks(G["wq"], p["wq"], CH)
                for k in ("wk", "wkd", "wv", "wvd"):
                    load_chunks(G[k], p[k], CCH)
                load(G["wg"][:, :], p["wg"])
                for k, name in enumerate(("bg", "al", "dl")):
                    load(G["sc"][:, k:k + 1], p[name].rearrange("(a d) -> a d", a=1).broadcast_to([P, 1]))
            s.n_loads = n

        G = {}
        o = 0

        def take(name, n, pattern=None, **kw):
            nonlocal o
            ap = M.heads[:, o:o + n]
            G[name] = ap.rearrange(pattern, **kw) if pattern else ap
            o += n
        take("wq", 3 * 640, "p (c f) -> p c f", c=3)
        take("wk", 2 * 640, "p (c f) -> p c f", c=2)
        take("wkd", 2 * 640, "p (c f) -> p c f", c=2)
        take("wv", 2 * D, "p (c f) -> p c f", c=2)
        take("wvd", 2 * D, "p (c f) -> p c f", c=2)
        take("QP", 5 * N, "p (c n) -> p c n", c=5)
        take("wg", 2)
        take("sc", 4)
        take("gv", 32)
        take("ctD", 2 * P, "p (c n) -> p c n", c=2)
        take("ctA", 2 * P, "p (c n) -> p c n", c=2)
        take("wgb", 2 * P, "p (c n) -> p c n", c=2)
        o2 = 0
        for name, n, pat, kw in (("Kbd", 5 * P, "p (c k) -> p c k", dict(c=5)), ("Vbd", 5 * 64, "p (c k) -> p c k", dict(c=5)),
                                 ("S", 640, "p (g k) -> p g k", dict(g=40)), ("PT", 640, "p (c n) -> p c n", dict(c=5)),
                                 ("mx", 40, None, {}), ("sum", 40, None, {}), ("fac", 40, None, {})):
            ap = M.values[:, o2:o2 + n]
            G[name] = ap.rearrange(pat, **kw) if pat else ap
            o2 += n

        def norm_dve(dve, s, b):
            if not s.prm["ln"]:
                return
            for t in range(TB):
                nc.vector.bn_stats(M.stats[:, t, :], M.x[:, (b - s.first) * TB + t, :]).then_inc(s.sem("stats"), 1)
            hold(dve, s.sem("stats"), after(b, TB, TB))
            for t in range(TB):
                nc.vector.bn_aggr(M.mv[:, t, :], M.stats[:, t, :]).then_inc(s.sem("mv"), 1)
            dve.wait_ge(s.sem("rstd"), after(b, 1, 1))
            for t in range(TB):
                nc.vector.tensor_scalar(M.xn[:, t, :], M.x[:, (b - s.first) * TB + t, :], M.mv[:, t, 0:1], M.rstd[:, t:t + 1],
                                        ALU.subtract, ALU.mult).then_inc(s.sem("xn"), 1)

        def norm_pool(pool, s, b):
            if s.prm["ln"]:
                hold(pool, s.sem("mv"), after(b, TB, TB))
                nc.gpsimd.tensor_scalar(M.vare[:, :], M.mv[:, :, 1], EPS, 1.0, ALU.add, ALU.mult).then_inc(s.sem("vare"), 1)
                hold(pool, s.sem("vare"), after(b, 1, 1))
                nc.gpsimd.tensor_tensor(M.rstd[:, :], M.vare[:, :], M.mhalf[:, :], ALU.pow).then_inc(s.sem("rstd"), 1)
            else:
                for t in range(TB):
                    nc.gpsimd.tensor_copy(M.xn[:, t, :], M.x[:, (b - s.first) * TB + t, :]).then_inc(s.sem("xn"), 1)

        def inputs_pe(pe, s, b):
            pe.wait_ge(s.sem("xn"), after(b, TB, TB))
            k = 0
            for a, w in CH:
                if k >= 2:
                    hold(pe, s.sem("in_evac" + s.tag), after(b - s.first, n_in(s), k - 1))
                for t in range(TB):
                    last = nc.tensor.transpose(M.PJ[k % 2][0:w, t * P:t * P + P], M.xn[:, t, a:a + w], M.ident[:, :])
                last.then_inc(s.sem("in_ps" + s.tag), 1)
                k += 1
            if s.prm["cross"]:
                pe.wait_ge(s.sem("ctx_in" + s.tag), after(b - s.first, 16, 16))
                for a, w in CCH:
                    hold(pe, s.sem("in_evac" + s.tag), after(b - s.first, n_in(s), k - 1))
                    for t in range(TB):
                        last = nc.tensor.transpose(M.PJ[k % 2][0:w, t * P:t * P + P], M.ctx_in[:, t, a:a + w], M.ident[:, :])
                    last.then_inc(s.sem("in_ps" + s.tag), 1)
                    k += 1

        def n_in(s):
            return 5 if s.prm["cross"] else 3

        def inputs_act(act, s, b):
            k = 0
            for c, (a, w) in enumerate(CH):
                act.wait_ge(s.sem("in_ps" + s.tag), after(b - s.first, n_in(s), k + 1))
                if s.prm["ln"]:
                    if c == 0:
                        act.wait_ge(s.w_in, 16 * s.n_loads)
                    ins = nc.scalar.activation(M.hT[0:w, c, :], M.PJ[k % 2][0:w, :], ACT.Identity,
                                               bias=M.b_col[0:w, c:c + 1], scale=M.g_col[0:w, c:c + 1])
                else:
                    ins = nc.scalar.copy(M.hT[0:w, c, :], M.PJ[k % 2][0:w, :])
                ins.then_inc(s.sem("in_evac" + s.tag), 1)
                k += 1
            if s.prm["cross"]:
                for c, (a, w) in enumerate(CCH):
                    act.wait_ge(s.sem("in_ps" + s.tag), after(b - s.first, n_in(s), k + 1))
                    nc.scalar.copy(M.cT[0:w, c, :], M.PJ[k % 2][0:w, :]).then_inc(s.sem("in_evac" + s.tag), 1)
                    k += 1

        def kvT(s):
            return M.cT if s.prm["cross"] else M.hT

        def out_pe(pe, s, b):
            v, chunks = V[s.name], out_chunks(s)
            nch = len(chunks)
            if s.kind != "ff":
                for c, (a, w) in enumerate(chunks):
                    if c >= 2:
                        hold(pe, s.sem("ot"), after(b, nch, c - 1))
                    for t in range(TB):
                        last = nc.tensor.transpose(M.PJ[c % 2][0:w, t * P:t * P + P], v["On"][:, t, a:a + w], M.ident[:, :])
                    last.then_inc(s.sem("ot_ps"), 1)
            pe.wait_ge(s.sem("ot"), after(b, nch, nch))
            for t in range(TB):
                if t >= 2:
                    pe.wait_ge(x_done, after(b, TB, (s.index * B - s.first) * TB + X_IN + t - 1))
                for c, (a, w) in enumerate(chunks):
                    last = nc.tensor.matmul(M.SM[t % 2][:, 0:D], v["OT"][0:w, c, t * P:t * P + P], v["wo"][0:w, c, :],
                                            start=c == 0, stop=c == nch - 1)
                last.then_inc(s.sem("y"), 1)

        def out_act(act, s, b):
            v, chunks = V[s.name], out_chunks(s)
            for c, (a, w) in enumerate(chunks):
                act.wait_ge(s.sem("ot_ps"), after(b, len(chunks), c + 1))
                nc.scalar.copy(v["OT"][0:w, c, :], M.PJ[c % 2][0:w, :]).then_inc(s.sem("ot"), 1)

        def out_dve(dve, s, b):
            for t in range(TB):
                dve.wait_ge(s.sem("y"), after(b, TB, t + 1))
                nc.vector.tensor_tensor(M.ysum[:, t % 2, :], M.SM[t % 2][:, 0:D], M.bo_row[:, :], ALU.add).then_inc(s.sem("ysum"), 1)
                dve.wait_ge(s.sem("ysum"), after(b, TB, t + 1))
                nc.vector.tensor_tensor(M.x[:, (b - s.first) * TB + t, :], M.ysum[:, t % 2, :], M.x[:, (b - s.first) * TB + t, :],
                                        ALU.add).then_inc(x_done, 1)

        def v_slices(s):
            return [(0, 8), (8, 8), (16, 4)] if s.prm["big"] else [(0, 20)]

        def values_pe(pe, s, b):
            v, dh, sl, kv = V[s.name], s.prm["dh"], v_slices(s), kv_chunks(s)
            pe.wait_ge(s.w_in, 16 * s.n_loads)
            hold(pe, s.sem("in_evac" + s.tag), after(b - s.first, n_in(s), n_in(s)))
            k = 0
            for t in range(TB):
                for h0, nh in sl:
                    if k >= 2:
                        pe.wait_ge(s.sem("v"), after(b, TB * len(sl), k - 1))
                    for c, (a, w) in enumerate(kv):
                        last = nc.tensor.matmul(M.PJ[k % 2][:, 0:nh * dh], kvT(s)[0:w, c, t * P:t * P + P],
                                                v["wv"][0:w, c, h0 * dh:(h0 + nh) * dh], start=c == 0, stop=c == len(kv) - 1)
                    last.then_inc(s.sem("v_ps"), 1)
                    k += 1

        def values_act(act, s, b):
            v, dh, sl = V[s.name], s.prm["dh"], v_slices(s)
            k = 0
            for t in range(TB):
                for h0, nh in sl:
                    act.wait_ge(s.sem("v_ps"), after(b, TB * len(sl), k + 1))
                    nc.scalar.copy(v["V"][:, t, h0:h0 + nh, 0:dh],
                                   M.PJ[k % 2][:, 0:nh * dh].rearrange("p (h d) -> p h d", h=nh)).then_inc(s.sem("v"), 1)
                    k += 1

        def stack_pe(pe, s, b):
            v = V[s.name]
            nv = TB * len(v_slices(s))
            hold(pe, s.sem("v"), after(b, nv, nv))
            for k in range(6):
                c, (a, w) = k // 2, CH[k // 2]
                if k >= 2:
                    pe.wait_ge(s.sem("rest"), after(b, 6, k - 1))
                wt, src, ch = (v["wq"], M.hT, CH) if k % 2 == 0 else (v["wk"], kvT(s), kv_chunks(s))
                for e, (_, ew) in enumerate(ch):
                    last = nc.tensor.matmul(M.PJ[k % 2][0:w, :], wt[0:ew, e, a:a + w], src[0:ew, e, :], start=e == 0, stop=e == len(ch) - 1)
                last.then_inc(s.sem("qk_ps"), 1)

        def stack_act(act, s, b):
            v = V[s.name]
            for k in range(6):
                w = CH[k // 2][1]
                act.wait_ge(s.sem("qk_ps"), after(b, 6, k + 1))
                if k >= 2:
                    act.wait_ge(s.sem(f"stack{k % 2}"), after(b, 3 * 96, 96 * (k // 2)))
                nc.scalar.copy(v["parts"][0:w, k % 2, 0, :], M.PJ[k % 2][0:w, :]).then_inc(s.sem("hi"), 1)

        def stack_dve(dve, s, b):
            v = V[s.name]
            for k in range(6):
                w = CH[k // 2][1]
                dve.wait_ge(s.sem("hi"), after(b, 6, k + 1))
                if k >= 2:
                    dve.wait_ge(s.sem("lo"), after(b, 6, k - 1))
                nc.vector.tensor_tensor(v["rest"][0:w, k % 2, :], M.PJ[k % 2][0:w, :], v["parts"][0:w, k % 2, 0, :],
                                        ALU.subtract).then_inc(s.sem("rest"), 1)

        def stack_pool(pool, s, b):
            v = V[s.name]
            for k in range(6):
                w = CH[k // 2][1]
                hold(pool, s.sem("rest"), after(b, 6, k + 1))
                if k >= 2:
                    hold(pool, s.sem(f"stack{k % 2}"), after(b, 3 * 96, 96 * (k // 2)))
                nc.gpsimd.tensor_copy(v["parts"][0:w, k % 2, 1, :], v["rest"][0:w, k % 2, :]).then_inc(s.sem("mid"), 1)
                hold(pool, s.sem("mid"), after(b, 6, k + 1))
                nc.gpsimd.tensor_tensor(v["parts"][0:w, k % 2, 2, :], v["rest"][0:w, k % 2, :], v["parts"][0:w, k % 2, 1, :],
                                        ALU.subtract).then_inc(s.sem("lo"), 1)

        def stack_sync(sp, s, b):
            v = V[s.name]
            for k in range(6):
                c, (a, w) = k // 2, CH[k // 2]
                nh = w // 16
                dst, order = (v["QS"], Q_PARTS) if k % 2 == 0 else (v["KS"], K_PARTS)
                sp.wait_ge(s.sem("lo"), after(b, 6, k + 1))
                for j, part in enumerate(order):
                    sp.dma_start(dst[16 * j:16 * j + 16, 8 * c:8 * c + nh, :],
                                 v["parts"][0:w, k % 2, "hml".index(part), :]).then_inc(s.sem(f"stack{k % 2}"), 16)

        def slot_loads(u):
            return sum(1 for x in range(u) if x % 2 == u % 2)

        def project_pe(pe, s, n, u, which):
            v = V[s.name]
            ch = CH if which == "q" else kv_chunks(s)
            src = M.hT if which == "q" else kvT(s)
            bank, off = (M.PJ[0], 0) if which == "q" else (M.PJ[1], 3)
            if which == "q":
                per = 16 * (3 if u % 2 == 0 else 2)
                pe.wait_ge(s.sem(f"wqk{u % 2}"), after(n, per, 16 * (slot_loads(u) + 1)))
            pe.wait_ge(s.sem(which + "_evac"), seeded(n, PAIRS, u))
            for e, (_, ew) in enumerate(ch):
                last = nc.tensor.matmul(bank[:, :], v["wqk"][0:ew, u % 2, off + e, :], src[0:ew, e, :], start=e == 0, stop=e == len(ch) - 1)
            last.then_inc(s.sem(which + "_ps"), 1)

        def project_act(act, s, n, u, which):
            v = V[s.name]
            act.wait_ge(s.sem(which + "_ps"), seeded(n, PAIRS, u + 1))
            act.wait_ge(s.sem("st"), seeded(n, 8 * PAIRS, 8 * (u - 1)))
            bank = M.PJ[0] if which == "q" else M.PJ[1]
            nc.scalar.copy(v["QT" if which == "q" else "KT"][:, u % 2, :], bank[:, :])
            nc.scalar.copy(v["QB" if which == "q" else "KB"][:, u % 2, :], bank[:, :]).then_inc(s.sem(which + "_evac"), 1)

        def rows_pe(pe, s, n, i, u, t):
            v = V[s.name]
            g, qb = t // TB, t % TB
            k = 8 * u + t
            if s.prm["big"] and t == 0:
                pe.wait_ge(s.sem("q_evac"), seeded(n, PAIRS, u + 1))
                pe.wait_ge(s.sem("k_evac"), seeded(n, PAIRS, u + 1))
            pe.wait_ge(s.sem("max"), seeded(n, 8 * PAIRS, k - 1))
            if s.prm["big"]:
                lhs = v["QB"][64 * g:64 * g + 64, u % 2, qb * P:qb * P + P]
                rhs = v["KB"][64 * g:64 * g + 64, u % 2, :]
            else:
                h = i * HPI + 2 * u + g
                lhs = v["QS"][0:96, h, qb * P:qb * P + P]
                rhs = v["KS"][0:96, h, :]
            nc.tensor.matmul(M.SM[t % 2][:, :], lhs, rhs, start=True, stop=True).then_inc(s.sem("rows"), 1)

        def max_dve(dve, s, n, u, t):
            if t == 0:
                dve.wait_ge(s.sem("nm_ps"), seeded(n, PAIRS, u - 1))
            dve.wait_ge(s.sem("rows"), seeded(n, 8 * PAIRS, 8 * u + t + 1))
            nc.vector.tensor_reduce(M.negm[:, u % 2, t % TB, t // TB:t // TB + 1], M.SM[t % 2][:, :], AX.X, ALU.max,
                                    negate=True).then_inc(s.sem("max"), 1)

        def negm_pe(pe, s, n, u):
            pe.wait_ge(s.sem("max"), seeded(n, 8 * PAIRS, 8 * u + 8))
            pe.wait_ge(s.sem("nm_lo"), seeded(n, PAIRS, u))
            for qb in range(TB):
                last = nc.tensor.transpose(M.TR[0:2, qb * P:qb * P + P], M.negm[:, u % 2, qb, :], M.ident[:, :])
            last.then_inc(s.sem("nm_ps"), 1)

        def negm_act(act, s, n, u):
            act.wait_ge(s.sem("nm_ps"), seeded(n, PAIRS, u + 1))
            act.wait_ge(s.sem("st"), seeded(n, 8 * PAIRS, 8 * (u - 1)))
            for g in range(2):
                last = nc.scalar.copy(M.nmT[64 * g:64 * g + 2, u % 2, :], M.TR[0:2, :])
            last.then_inc(s.sem("nm_hi"), 1)

        def negm_dve(dve, s, n, u):
            dve.wait_ge(s.sem("nm_hi"), seeded(n, PAIRS, u + 1))
            for g in range(2):
                last = nc.vector.tensor_tensor(M.nmT[64 * g + 32:64 * g + 34, u % 2, :], M.TR[0:2, :], M.nmT[0:2, u % 2, :], ALU.subtract)
            last.then_inc(s.sem("nm_lo"), 1)

        def columns_pe(pe, s, n, i, u, t):
            v = V[s.name]
            g, kb = t // TB, t % TB
            k = 8 * u + t
            pe.wait_ge(s.sem("exp"), seeded(n, 8 * PAIRS, k - 1))
            if s.prm["big"]:
                lhs = v["KT"][64 * g:64 * g + 64, u % 2, kb * P:kb * P + P]
                rhs = v["QT"][64 * g:64 * g + 64, u % 2, :]
            else:
                h = i * HPI + 2 * u + g
                lhs = v["KS"][0:96, h, kb * P:kb * P + P]
                rhs = v["QS"][0:96, h, :]
            nc.tensor.matmul(M.ST[t % 2][:, :], lhs, rhs, start=True, stop=False)
            if t == 0:
                pe.wait_ge(s.sem("nm_lo"), seeded(n, PAIRS, u + 1))
            strip = slice(64 * g, 64 * g + 34)
            nc.tensor.matmul(M.ST[t % 2][:, :], M.sel[strip, :], M.nmT[strip, u % 2, :], start=False, stop=True).then_inc(s.sem("st"), 1)

        def exp_act(act, s, n, u, t):
            h, kb = 2 * u + t // TB, t % TB
            act.wait_ge(s.sem("st"), seeded(n, 8 * PAIRS, 8 * u + t + 1))
            if kb == 0:
                act.wait_ge(s.sem("av"), seeded(n, HPI, h - 1))
            nc.scalar.activation(M.probs[:, h % 2, kb, :], M.ST[t % 2][:, :], ACT.Exp,
                                 scale=float(s.prm["dh"]) ** -0.5).then_inc(s.sem("exp"), 1)

        def mix_pe(pe, s, n, i, h, qb):
            v, dh = V[s.name], s.prm["dh"]
            if qb == 0:
                pe.wait_ge(s.sem("exp"), seeded(n, 8 * PAIRS, TB * (h + 1)))
                pe.wait_ge(s.sem("on"), seeded(n, HPI, h))
            for kb in range(TB):
                last = nc.tensor.matmul(M.OB[:, qb * (dh + 1):(qb + 1) * (dh + 1)], M.probs[:, h % 2, kb, qb * P:qb * P + P],
                                        v["V"][:, kb, i * HPI + h, :], start=kb == 0, stop=kb == TB - 1)
            if qb == TB - 1:
                last.then_inc(s.sem("av"), 1)

        def mix_dve(dve, s, n, i, h):
            v, dh = V[s.name], s.prm["dh"]
            ob = M.OB[:, 0:TB * (dh + 1)].rearrange("p (t d) -> p t d", t=TB)
            dve.wait_ge(s.sem("av"), seeded(n, HPI, h + 1))
            nc.vector.reciprocal(M.rec[:, h % 2, :], ob[:, :, dh]).then_inc(s.sem("rec"), 1)
            dve.wait_ge(s.sem("rec"), seeded(n, HPI, h + 1))
            nc.vector.tensor_tensor(v["On"][:, :, bass.ts(i * HPI + h, dh)], ob[:, :, 0:dh],
                                    M.rec[:, h % 2, :].unsqueeze(2).broadcast_to([P, TB, dh]), ALU.mult).then_inc(s.sem("on"), 1)

        def attention_pe(pe, s):
            with pe.Fori(s.first, s.first + B) as b:
                start(pe, s, b)
                inputs_pe(pe, s, b)
                values_pe(pe, s, b)
                nv = TB * len(v_slices(s))
                if s.prm["big"]:
                    hold(pe, s.sem("v"), after(b, nv, nv))
                else:
                    stack_pe(pe, s, b)
                    for k in range(2):
                        hold(pe, s.sem(f"stack{k}"), after(b, 3 * 96, 3 * 96))
                with pe.Fori(0, ITERS) as i:
                    n = pe.snap(b * ITERS + i)
                    if s.prm["big"]:
                        project_pe(pe, s, n, 0, "q")
                        project_pe(pe, s, n, 0, "k")
                    for t in range(8):
                        rows_pe(pe, s, n, i, 0, t)
                    for u in range(PAIRS):
                        more = u + 1 < PAIRS
                        if s.prm["big"] and more:
                            project_pe(pe, s, n, u + 1, "q")
                        negm_pe(pe, s, n, u)
                        if s.prm["big"] and more:
                            project_pe(pe, s, n, u + 1, "k")
                        for t in range(8):
                            columns_pe(pe, s, n, i, u, t)
                            if more:
                                rows_pe(pe, s, n, i, u + 1, t)
                            h = 2 * u - 1 + t // TB
                            if h >= 0:
                                mix_pe(pe, s, n, i, h, t % TB)
                    for qb in range(TB):
                        mix_pe(pe, s, n, i, HPI - 1, qb)
                pe.wait_ge(s.sem("on"), seeded(b, ITERS * HPI, ITERS * HPI))
                out_pe(pe, s, b)

        def attention_act(act, s):
            with act.Fori(s.first, s.first + B) as b:
                start(act, s, b)
                inputs_act(act, s, b)
                values_act(act, s, b)
                if not s.prm["big"]:
                    stack_act(act, s, b)
                with act.Fori(0, ITERS) as i:
                    n = act.snap(b * ITERS + i)
                    if s.prm["big"]:
                        project_act(act, s, n, 0, "q")
                        project_act(act, s, n, 0, "k")
                    for u in range(PAIRS):
                        more = s.prm["big"] and u + 1 < PAIRS
                        if more:
                            project_act(act, s, n, u + 1, "q")
                        negm_act(act, s, n, u)
                        if more:
                            project_act(act, s, n, u + 1, "k")
                        for t in range(8):
                            exp_act(act, s, n, u, t)
                out_act(act, s, b)

        def attention_dve(dve, s):
            start(dve, s, s.first)
            nc.vector.memset(V[s.name]["V"][:, :, :, s.prm["dh"]], 1.0)
            with dve.Fori(s.first, s.first + B) as b:
                start(dve, s, b)
                norm_dve(dve, s, b)
                if not s.prm["big"]:
                    stack_dve(dve, s, b)
                with dve.Fori(0, ITERS) as i:
                    n = dve.snap(b * ITERS + i)
                    for t in range(8):
                        max_dve(dve, s, n, 0, t)
                    for u in range(PAIRS):
                        negm_dve(dve, s, n, u)
                        for t in range(8):
                            if u + 1 < PAIRS:
                                max_dve(dve, s, n, u + 1, t)
                            if t == TB - 1 and u > 0:
                                mix_dve(dve, s, n, i, 2 * u - 1)
                            if t == 7:
                                mix_dve(dve, s, n, i, 2 * u)
                    mix_dve(dve, s, n, i, HPI - 1)
                dve.wait_ge(s.w_in, 16 * s.n_loads)
                out_dve(dve, s, b)

        def attention_pool(pool, s):
            with pool.Fori(s.first, s.first + B) as b:
                start(pool, s, b)
                norm_pool(pool, s, b)
                if s.kind == "att" and not s.prm["big"]:
                    stack_pool(pool, s, b)

        def load_context(sp, s, b):
            sp.dma_start(M.ctx_in[:, :, :], io["ctx"][bass.ts(b - s.first, N), :].rearrange("(t p) d -> p t d", p=P)).then_inc(s.sem("ctx_in" + s.tag), 16)

        def attention_sync(sp, s):
            load_weights(sp, s)
            nk = len(kv_chunks(s))
            with sp.Fori(s.first, s.first + B) as b:
                start(sp, s, b)
                if s.prm["cross"]:
                    load_context(sp, s, b)
                if s.prm["big"]:
                    with sp.Fori(0, ITERS) as i:
                        n = sp.snap(b * ITERS + i)
                        for u in range(PAIRS):
                            sp.wait_ge(s.sem("k_ps"), seeded(n, PAIRS, u - 1))
                            sp.dma_start(V[s.name]["wqk"][:, u % 2, :, :],
                                         s.prm["wqk"][bass.ts(i * PAIRS + u, P), :].rearrange("p (c f) -> p c f", f=P)
                                         ).then_inc(s.sem(f"wqk{u % 2}"), 16)
                else:
                    stack_sync(sp, s, b)

        NF = DFF // P

        def ff_pe(pe, s):
            v = V[s.name]
            with pe.Fori(s.first, s.first + B) as b:
                start(pe, s, b)
                inputs_pe(pe, s, b)
                pe.wait_ge(s.w_in, 16 * s.n_loads)
                hold(pe, s.sem("in_evac" + s.tag), after(b - s.first, 3, 3))
                for j in range(NF):
                    if j >= 2:
                        pe.wait_ge(s.sem("ot"), after(b, NF, j - 1))
                    for half, bank in ((1, M.ST[j % 2]), (0, M.PJ[j % 2])):
                        for e, (_, w) in enumerate(CH):
                            last = nc.tensor.matmul(bank[:, :], v["w1"][0:w, e, half * DFF + j * P:half * DFF + j * P + P],
                                                    M.hT[0:w, e, :], start=e == 0, stop=e == 2)
                        last.then_inc(s.sem("a_ps" if half == 0 else "g_ps"), 1)
                out_pe(pe, s, b)

        def ff_act(act, s):
            v = V[s.name]
            with act.Fori(s.first, s.first + B) as b:
                start(act, s, b)
                inputs_act(act, s, b)
                for j in range(NF):
                    act.wait_ge(s.sem("g_ps"), after(b, NF, j + 1))
                    if j >= 2:
                        act.wait_ge(s.sem("ot"), after(b, NF, j - 1))
                    nc.scalar.activation(v["gate"][:, j % 2, :], M.ST[j % 2][:, :], s.prm["gelu"],
                                         bias=M.b1_col[:, NF + j:NF + j + 1]).then_inc(s.sem("gelu"), 1)

        def ff_dve(dve, s):
            v = V[s.name]
            with dve.Fori(s.first, s.first + B) as b:
                start(dve, s, b)
                norm_dve(dve, s, b)
                dve.wait_ge(s.w_in, 16 * s.n_loads)
                for j in range(NF):
                    dve.wait_ge(s.sem("gelu"), after(b, NF, j + 1))
                    dve.wait_ge(s.sem("a_ps"), after(b, NF, j + 1))
                    nc.vector.scalar_tensor_tensor(out=v["OT"][:, j, :], in0=M.PJ[j % 2][:, :], scalar=M.b1_col[:, j:j + 1],
                                                   in1=v["gate"][:, j % 2, :], op0=ALU.add, op1=ALU.mult).then_inc(s.sem("ot"), 1)
                out_dve(dve, s, b)

        def gated_pe(pe, s):
            v = V[s.name]
            A, Bk = M.ST[0], M.ST[1]
            with pe.Fori(s.first, s.first + B) as b:
                start(pe, s, b)
                inputs_pe(pe, s, b)
                pe.wait_ge(s.w_in, 16 * s.n_loads)
                hold(pe, s.sem("in_evac" + s.tag), after(b - s.first, 5, 5))
                for c in range(5):
                    if c >= 2:
                        pe.wait_ge(s.sem("qp"), after(b, 5, c - 1))
                    for e, (_, w) in enumerate(CH):
                        last = nc.tensor.matmul(M.PJ[c % 2][:, :], G["wq"][0:w, e, c * P:c * P + P], M.hT[0:w, e, :], start=e == 0, stop=e == 2)
                    last.then_inc(s.sem("qp_ps"), 1)
                pe.wait_ge(s.sem("tok"), after(b, 4, 4))
                for c in range(5):
                    for e, (_, w) in enumerate(CCH):
                        nc.tensor.matmul(M.SM[0][:, c * 32:c * 32 + 32], G["wkd"][0:w, e, c * P:c * P + P], G["ctD"][0:w, e, 0:32],
                                         start=e == 0, stop=False)
                    for e, (_, w) in enumerate(CCH):
                        last = nc.tensor.matmul(M.SM[0][:, c * 32:c * 32 + 32], G["wk"][0:w, e, c * P:c * P + P], G["ctA"][0:w, e, 0:32],
                                                start=False, stop=e == 1)
                for e, (_, w) in enumerate(CCH):
                    last = nc.tensor.matmul(M.SM[0][:, 256:256 + NTOK], G["wgb"][0:w, e, :], G["ctD"][0:w, e, 0:NTOK],
                                            start=e == 0, stop=e == 1)
                last.then_inc(s.sem("k_ps"), 1)
                for src, wt, first in (("ctD", "wvd", True), ("ctA", "wv", False)):
                    for e, (_, w) in enumerate(CCH):
                        last = nc.tensor.matmul(M.SM[1][:, 0:D], G[src][0:w, e, :], G[wt][0:w, e, :],
                                                start=first and e == 0, stop=(not first) and e == 1)
                last.then_inc(s.sem("v_ps"), 1)
                pe.wait_ge(s.sem("qp"), after(b, 5, 5))
                pe.wait_ge(s.sem("kbd"), after(b, 4, 4))
                pe.wait_ge(s.sem("vbd"), after(b, 4, 4))
                for qb in range(TB):
                    if qb:
                        pe.wait_ge(s.sem("sub"), after(b, 2 * TB, 2 * qb))
                    for c in range(5):
                        last = nc.tensor.matmul((A if c < 4 else Bk)[:, (c % 4) * P:(c % 4) * P + P], G["QP"][:, c, qb * P:qb * P + P],
                                                G["Kbd"][:, c, :], start=True, stop=True)
                    last.then_inc(s.sem("s_ps"), 1)
                    pe.wait_ge(s.sem("p"), after(b, TB, qb + 1))
                    for c in range(5):
                        last = nc.tensor.transpose((M.PJ[0] if c < 4 else M.PJ[1])[:, (c % 4) * P:(c % 4) * P + P],
                                                   G["S"][:, 8 * c:8 * c + 8, :], M.ident[:, :])
                    last.then_inc(s.sem("pt_ps"), 1)
                    pe.wait_ge(s.sem("pt"), after(b, 2 * TB, 2 * qb + 2))
                    if qb:
                        pe.wait_ge(s.sem("on"), after(b, TB, qb))
                    for c in range(5):
                        last = nc.tensor.matmul(M.OB[:, c * 64:c * 64 + 64], G["PT"][:, c, :], G["Vbd"][:, c, :], start=True, stop=True)
                    last.then_inc(s.sem("o_ps"), 1)
                pe.wait_ge(s.sem("on"), after(b, TB, TB))
                out_pe(pe, s, b)

        def gated_act(act, s):
            v = V[s.name]
            with act.Fori(s.first, s.first + B) as b:
                start(act, s, b)
                inputs_act(act, s, b)
                for c in range(5):
                    act.wait_ge(s.sem("qp_ps"), after(b, 5, c + 1))
                    nc.scalar.copy(G["QP"][:, c, :], M.PJ[c % 2][:, :]).then_inc(s.sem("qp"), 1)
                act.wait_ge(s.sem("arg"), after(b, 2, 2))
                nc.scalar.activation(G["gv"][:, 4:6], G["gv"][:, 2:4], ACT.Exp, scale=-1.0).then_inc(s.sem("ge"), 1)
                for qb in range(TB):
                    act.wait_ge(s.sem("sub"), after(b, 2 * TB, 2 * qb + 2))
                    nc.scalar.activation(G["S"][:, :, :], G["S"][:, :, :], ACT.Exp, scale=float(s.prm["dh"]) ** -0.5).then_inc(s.sem("e"), 1)
                    act.wait_ge(s.sem("pt_ps"), after(b, TB, qb + 1))
                    nc.scalar.copy(G["PT"][:, 0:4, :], M.PJ[0][:, :].rearrange("p (c n) -> p c n", c=4)).then_inc(s.sem("pt"), 1)
                    nc.scalar.copy(G["PT"][:, 4, :], M.PJ[1][:, 0:P]).then_inc(s.sem("pt"), 1)
                    act.wait_ge(s.sem("o_ps"), after(b, TB, qb + 1))
                    nc.scalar.copy(v["On"][:, qb, :], M.OB[:, 0:D]).then_inc(s.sem("on"), 1)
                out_act(act, s, b)

        def gated_pool(pool, s):
            with pool.Fori(s.first, s.first + B) as b:
                start(pool, s, b)
                norm_pool(pool, s, b)

        def gated_dve(dve, s):
            v = V[s.name]
            start(dve, s, s.first)
            z = s.sem("zero")
            nc.vector.memset(G["Kbd"][:, :, :], 0.0).then_inc(z, 1)
            nc.vector.memset(G["Vbd"][:, :, :], 0.0).then_inc(z, 1)
            nc.vector.memset(G["ctD"][:, :, :], 0.0).then_inc(z, 1)
            nc.vector.memset(G["ctA"][:, :, :], 0.0).then_inc(z, 1)
            nc.vector.memset(G["wgb"][:, :, :], 1.0).then_inc(z, 1)
            dve.wait_ge(z, 5)
            dve.wait_ge(s.w_in, 16 * s.n_loads)
            for e, (_, w) in enumerate(CCH):
                nc.vector.tensor_scalar(G["wgb"][0:w, e, :], G["wgb"][0:w, e, :], G["wg"][0:w, e:e + 1], None, ALU.mult)
            gv, sc, ch = G["gv"], G["sc"], s.sem("chain")
            with dve.Fori(s.first, s.first + B) as b:
                start(dve, s, b)
                dve.wait_ge(s.sem("in_evac" + s.tag), after(b - s.first, 5, 5))
                for e, (_, w) in enumerate(CCH):
                    for name, at in (("ctD", 0), ("ctA", NTOK)):
                        dst = G[name][0:w, e, :].rearrange("p (r k) -> p r k", r=4)[:, :, at:at + NTOK]
                        nc.vector.tensor_copy(dst, M.cT[0:w, e, at:at + NTOK].unsqueeze(1).broadcast_to([w, 4, NTOK])).then_inc(s.sem("tok"), 1)
                dve.wait_ge(s.sem("k_ps"), after(b, 1, 1))
                for g in range(4):
                    q = slice(32 * g, 32 * g + 32)
                    nc.vector.tensor_copy(G["Kbd"][q, :, q], M.SM[0][q, 0:160].rearrange("p (c k) -> p c k", c=5)).then_inc(s.sem("kbd"), 1)
                nc.vector.reduce_sum(gv[:, 0:1], M.SM[0][:, 256:256 + NTOK], AX.X).then_inc(ch, 1)
                dve.wait_ge(ch, after(b, 3 + 3 * TB, 1))
                nc.vector.tensor_scalar(gv[:, 1:2], gv[:, 0:1], 1.0 / NTOK, sc[:, 0:1], ALU.mult, ALU.add).then_inc(ch, 1)
                dve.wait_ge(ch, after(b, 3 + 3 * TB, 2))
                nc.vector.tensor_tensor(gv[:, 2:3], sc[:, 2:3], gv[:, 1:2], ALU.add).then_inc(s.sem("arg"), 1)
                nc.vector.tensor_tensor(gv[:, 3:4], sc[:, 1:2], gv[:, 1:2], ALU.subtract).then_inc(s.sem("arg"), 1)
                dve.wait_ge(s.sem("v_ps"), after(b, 1, 1))
                for g in range(4):
                    q = slice(32 * g, 32 * g + 32)
                    nc.vector.tensor_copy(G["Vbd"][q, :, 16 * g:16 * g + 16],
                                          M.SM[1][q, 0:D].rearrange("p (c k) -> p c k", c=5)[:, :, 16 * g:16 * g + 16]).then_inc(s.sem("vbd"), 1)
                dve.wait_ge(s.sem("ge"), after(b, 1, 1))
                nc.vector.tensor_scalar(gv[:, 6:8], gv[:, 4:6], 1.0, None, ALU.add).then_inc(ch, 1)
                dve.wait_ge(ch, after(b, 3 + 3 * TB, 3))
                nc.vector.reciprocal(gv[:, 8:10], gv[:, 6:8]).then_inc(s.sem("gate"), 1)
                for qb in range(TB):
                    dve.wait_ge(s.sem("s_ps"), after(b, TB, qb + 1))
                    if qb:
                        dve.wait_ge(s.sem("pt_ps"), after(b, TB, qb))
                    banks = ((M.ST[0][:, :], 0, 32), (M.ST[1][:, 0:P], 32, 8))
                    for src, g0, ng in banks:
                        last = nc.vector.reduce_max(G["mx"][:, g0:g0 + ng], src.rearrange("p (g k) -> p g k", k=NTOK), AX.X)
                        last.then_inc(s.sem("mx"), 1)
                    dve.wait_ge(s.sem("mx"), after(b, 2 * TB, 2 * qb + 2))
                    for src, g0, ng in banks:
                        nc.vector.tensor_tensor(G["S"][:, g0:g0 + ng, :], src.rearrange("p (g k) -> p g k", k=NTOK),
                                                G["mx"][:, g0:g0 + ng].unsqueeze(2).broadcast_to([P, ng, NTOK]), ALU.subtract).then_inc(s.sem("sub"), 1)
                    dve.wait_ge(s.sem("e"), after(b, TB, qb + 1))
                    nc.vector.reduce_sum(G["sum"][:, :], G["S"][:, :, :], AX.X).then_inc(ch, 1)
                    dve.wait_ge(ch, after(b, 3 + 3 * TB, 3 + 3 * qb + 1))
                    nc.vector.reciprocal(G["fac"][:, :], G["sum"][:, :]).then_inc(ch, 1)
                    dve.wait_ge(ch, after(b, 3 + 3 * TB, 3 + 3 * qb + 2))
                    dve.wait_ge(s.sem("gate"), after(b, 1, 1))
                    nc.vector.tensor_tensor(G["sum"][:, :].rearrange("p (h k) -> p h k", k=2), G["fac"][:, :].rearrange("p (h k) -> p h k", k=2),
                                            gv[:, 8:10].unsqueeze(1).broadcast_to([P, HEADS, 2]), ALU.mult).then_inc(ch, 1)
                    dve.wait_ge(ch, after(b, 3 + 3 * TB, 3 + 3 * qb + 3))
                    nc.vector.tensor_tensor(G["S"][:, :, :], G["S"][:, :, :], G["sum"][:, :].unsqueeze(2).broadcast_to([P, 40, NTOK]),
                                            ALU.mult).then_inc(s.sem("p"), 1)
                out_dve(dve, s, b)

        def simple_sync(sp, s):
            load_weights(sp, s)
            if s.prm["cross"]:
                with sp.Fori(s.first, s.first + B) as b:
                    start(sp, s, b)
                    load_context(sp, s, b)

        block = ctx.enter_context(nc.Block())

        @block.sync
        def _(sp):
            sp.dma_start(M.x[:, :, :], io["x"].rearrange("(t p) d -> p t d", p=P)).then_inc(x_done, X_IN)
            for s in (wide, narrow):
                for what in SEEDED:
                    if s is wide or what[0:2] not in ("q_", "k_"):
                        sp.sem_inc(s.sem(what), 1)
            for s in stages:
                (attention_sync if s.kind == "att" else simple_sync)(sp, s)
            sp.wait_ge(x_done, X_IN + len(stages) * NX)
            sp.dma_start(io["out"].rearrange("(t p) d -> p t d", p=P), M.x[:, :, :]).then_inc(x_out, 16)
            sp.wait_ge(x_out, 16)

        @block.gpsimd
        def _(pool):
            nc.gpsimd.memset(M.mhalf[:, :], -0.5)
            nc.gpsimd.memset(M.ident[:, :], 0.0).then_inc(consts0, 1)
            nc.gpsimd.memset(M.nmT[:, :, :], 0.0).then_inc(consts0, 1)
            nc.gpsimd.memset(M.sel[:, :], 0.0).then_inc(consts0, 1)
            pool.wait_ge(consts0, 3)
            nc.gpsimd.affine_select(out=M.ident[:, :], in_=M.ident[:, :], compare_op=ALU.not_equal, fill=1.0, base=0,
                                    pattern=[[-1, P]], channel_multiplier=1).then_inc(consts, 1)
            pool.wait_ge(consts, 1)
            for k, row in enumerate((0, 32, 64 + 1, 96 + 1)):
                quadrant = slice(32 * (row // 32), 32 * (row // 32) + 32)
                nc.gpsimd.affine_select(out=M.sel[quadrant, :], in_=M.sel[quadrant, :], compare_op=ALU.not_equal, fill=1.0,
                                        base=-(row % 32), pattern=[[0, P]], channel_multiplier=1).then_inc(consts, 1)
                pool.wait_ge(consts, k + 2)
            for s in stages:
                attention_pool(pool, s)

        @block.tensor
        def _(pe):
            pe.wait_ge(consts, 5)
            for s in stages:
                {"att": attention_pe, "ff": ff_pe, "gated": gated_pe}[s.kind](pe, s)

        @block.scalar
        def _(act):
            act.wait_ge(consts0, 3)
            for s in stages:
                {"att": attention_act, "ff": ff_act, "gated": gated_act}[s.kind](act, s)

        @block.vector
        def _(dve):
            dve.wait_ge(consts0, 3)
            for s in stages:
                {"att": attention_dve, "ff": ff_dve, "gated": gated_dve}[s.kind](dve, s)


def kernel(**inputs):
    import numpy as np
    import concourse.bacc as bacc
    from concourse.bass_utils import run_bass_kernel_spmd

    nc = bacc.Bacc("TRN2", target_bir_lowering=False, num_devices=1)
    arrays = {}

    def arr(name):
        return np.asarray(inputs[name])

    def put(name, a):
        a = np.ascontiguousarray(a)
        arrays[name] = a
        return nc.dram_tensor(name, a.shape, mybir.dt.from_np(a.dtype), kind="ExternalInput").ap()

    def pairs(tag, wq, wk):
        nk = -(-wk.shape[0] // P)
        out = np.zeros((10, P, 3 + nk, P), wq.dtype)
        for w, off in ((wq, 0), (wk, 3)):
            for c in range(-(-w.shape[0] // P)):
                rows = w[c * P:(c + 1) * P]
                out[:, 0:rows.shape[0], off + c, :] = rows.reshape(rows.shape[0], 10, P).transpose(1, 0, 2)
        return put(tag, out.reshape(10 * P, (3 + nk) * P))

    def spread(tag, w):
        out = np.zeros((w.shape[0], HEADS, 32), w.dtype)
        out[:, :, 0:16] = w.reshape(w.shape[0], HEADS, 16)
        return put(tag, out.reshape(w.shape[0], HEADS * 32))

    def columns(a):
        out = np.zeros((-(-a.size // P), P), a.dtype)
        out.reshape(-1)[0:a.size] = a.reshape(-1)
        return out.T

    def by_dimension(w):
        return np.concatenate([w[:, a:a + n].reshape(-1, n // 16, 16).transpose(0, 2, 1).reshape(-1, n) for a, n in CH], 1)

    def plain(prefix, **names):
        order = {"g": columns, "be": columns, "b1": columns, "wq": by_dimension, "wk": by_dimension}
        return {k: put(f"in_{prefix}{v}", order.get(k, lambda a: a)(arr(prefix + v))) for k, v in names.items()}

    L0, L1, L2, L3 = "L0_xattn_", "L1_xattn_", "L2_xattn_", "L3_xattn_"
    io = {
        "x": put("in_x", arr("x").reshape(B * N, D)),
        "ctx": put("in_ctx", arr("ctx_768").reshape(B * N, CD)),
        "L0a": plain(L0, g="g1", be="be1", wv="wv1", wo="wo1", bo="bo1") | {"wqk": pairs("in_wqk1", arr(L0 + "wq1"), arr(L0 + "wk1"))},
        "L0b": plain(L0, g="g2", be="be2", wv="wv2", wo="wo2", bo="bo2") | {"wqk": pairs("in_wqk2", arr(L0 + "wq2"), arr(L0 + "wk2"))},
        "L0f": plain(L0, g="g3", be="be3", w1="w_ff1", b1="b_ff1", wo="w_ff2", bo="b_ff2"),
        "L1a": plain(L1, g="n1_g", be="n1_b", wq="q1", wk="k1", wv="v1", wo="o1_w", bo="o1_b"),
        "L1b": plain(L1, g="n2_g", be="n2_b", wq="q2", wk="k2", wv="v2", wo="o2_w", bo="o2_b"),
        "L1f": plain(L1, g="n3_g", be="n3_b", w1="ff_w1", b1="ff_b1", wo="ff_w2", bo="ff_b2"),
        "L2": {
            "wq": spread("in_l2q", arr(L2 + "w_q").T), "wk": spread("in_l2k", arr(L2 + "w_k").T),
            "wkd": spread("in_l2kd", arr(L2 + "w_k_dis").T),
            "wv": put("in_l2v", arr(L2 + "w_v").T), "wvd": put("in_l2vd", arr(L2 + "w_v_dis").T),
            "wo": put("in_l2o", arr(L2 + "w_out").T), "bo": put("in_l2bo", arr(L2 + "b_out")),
            "wg": put("in_l2g", columns(arr(L2 + "w_gate"))), "bg": put("in_l2bg", arr(L2 + "b_gate").reshape(1)),
            "al": put("in_l2al", arr(L2 + "anat_gate_logit").reshape(1)), "dl": put("in_l2dl", arr(L2 + "dis_gate_logit").reshape(1)),
        },
        "L3": plain(L3, wq="Wq", wk="Wk", wv="Wv", wo="Wo", bo="bo"),
        "out": nc.dram_tensor("out_0", (B * N, D), F32, kind="ExternalOutput").ap(),
    }
    program(nc, io)
    result = run_bass_kernel_spmd(nc, [arrays], core_ids=[0])
    return result.results[0]["out_0"].reshape(B, N, D)
```

```python
from contextlib import ExitStack

import concourse.bass as bass
from concourse import mybir

F32 = mybir.dt.float32
BF16 = mybir.dt.bfloat16
ALU = mybir.AluOpType
ACT = mybir.ActivationFunctionType
AX = mybir.AxisListType

P = 128
B = 4
N = 512
TB = N // P
D = 320
CD = 192
HEADS = 20
DFF = 1280
EPS = 1e-5
CH = [(0, 128), (128, 128), (256, 64)]
CCH = [(0, 128), (128, 64)]
UNITS = HEADS * TB
X_IN = 16
NTOK = 16
Q_PARTS = "hmhlhm"
K_PARTS = "hhmhlm"


def after(n, per, k):
    return n * per + max(k, 0)


SEEDED = ("q_ps", "k_ps", "q_evac", "k_evac", "rows", "max", "nm_ps", "nm_hi", "nm_lo", "st", "exp", "av", "ob", "on", "psum",
          "den", "rcp", "ox_ps")


def seeded(n, per, k):
    return after(n, per, k) + 1


class Memory:

    def __init__(self, nc, ctx):
        def sb(name, shape, dt=F32):
            return ctx.enter_context(nc.sbuf_tensor(name, shape, dt))

        self.x = sb("x_res", [P, B * TB, D])
        self.weights = sb("weights", [P, 10944])
        self.heads = sb("heads", [P, 10752])
        self.values = sb("values", [P, 5200])
        self.mixed = sb("mixed", [P, 10 * N])
        self.probs = sb("probs", [P, 2, TB, N])
        self.xn = sb("xn", [P, TB, D])
        self.ctx_in = sb("ctx_in", [P, TB, CD])
        self.hT = sb("hT", [P, 3, N])
        self.cT = sb("cT", [P, 2, N])
        self.ident = sb("ident", [P, P])
        self.sel = sb("sel", [P, P], BF16)
        self.nmT = sb("nmT", [P, 2, N], BF16)
        self.ones = sb("ones", [P, 64])
        self.negm = sb("negm", [P, 3, TB, 4])
        self.rec = sb("rec", [P, N])
        self.ox = sb("ox", [P, N])
        self.stats = sb("stats", [P, TB, 6])
        self.mv = sb("mv", [P, TB, 2])
        self.rstd = sb("rstd", [P, TB])
        self.vare = sb("vare", [P, TB])
        self.mhalf = sb("mhalf", [P, TB])
        self.g_col = sb("g_col", [P, 3])
        self.b_col = sb("b_col", [P, 3])
        self.b1_col = sb("b1_col", [P, 2 * DFF // P])
        self.bo_row = sb("bo_row", [P, D])
        self.ysum = sb("ysum", [P, 2, D])
        self.small = sb("small", [P, 64])
        self.bank = [ctx.enter_context(nc.psum_tensor(f"bank{i}", [P, 512], F32)) for i in range(8)]
        self.PJ = self.bank[0:2]
        self.SM = self.bank[2:4]
        self.ST = self.bank[4:6]
        self.OB = self.bank[6]
        self.TR = self.bank[7]


class Stage:

    def __init__(self, nc, ctx, name, index, like=None, **kw):
        self.name, self.index, self.nc, self.ctx = name, index, nc, ctx
        self.sems = like.sems if like else {}
        self.first = like.first + B if like else 0
        self.kind = kw.pop("kind")
        self.prm = kw
        self.tag = name
        self.w_in = ctx.enter_context(nc.semaphore(f"{name}_w_in"))

    def sem(self, what):
        if what not in self.sems:
            self.sems[what] = self.ctx.enter_context(self.nc.semaphore(f"{self.name}_{what}"))
        return self.sems[what]


def program(nc, io):
    with ExitStack() as ctx:
        M = Memory(nc, ctx)
        stats, mv, vare, rstd, xn, xcopy = (ctx.enter_context(nc.semaphore(n)) for n in ("stats", "mv", "vare", "rstd", "xn", "xcopy"))
        x_done = ctx.enter_context(nc.semaphore("x_done"))
        consts = ctx.enter_context(nc.semaphore("consts"))
        consts0 = ctx.enter_context(nc.semaphore("consts0"))
        x_out = ctx.enter_context(nc.semaphore("x_out"))

        def att(name, i, big, ln, cross, **kw):
            return Stage(nc, ctx, name, i, kind="att", big=big, ln=ln, cross=cross, dh=64 if big else 16, group=2 if big else 4, **kw)

        ff0 = Stage(nc, ctx, "s2", 2, kind="ff", ln=True, cross=False, gelu=ACT.Gelu_apprx_tanh, **io["L0f"])
        wide = att("s0", 0, True, True, False, **io["L0a"])
        narrow = att("s3", 3, False, True, False, **io["L1a"])
        narrow2 = att("s4", 4, False, True, True, like=narrow, **io["L1b"])
        stages = [
            wide,
            att("s1", 1, True, True, True, like=wide, **io["L0b"]),
            ff0,
            narrow,
            narrow2,
            Stage(nc, ctx, "s5", 5, like=ff0, kind="ff", ln=True, cross=False, gelu=ACT.Gelu, **io["L1f"]),
            Stage(nc, ctx, "s6", 6, kind="gated", ln=False, cross=True, dh=16, **io["L2"]),
            att("s7", 7, False, False, True, like=narrow2, **io["L3"]),
        ]
        NX = B * TB

        def hold(eng, sem, value):
            eng.wait_ge(sem, value)
            eng.nop(nofuse=True)

        def start(eng, s, b):
            hold(eng, x_done, after(b, TB, (s.index * B - s.first) * TB + X_IN))

        def views(s):
            v = {}
            p = s.prm
            if s.kind == "ff":
                v["w1"] = M.weights[:, 0:3 * 2 * DFF].rearrange("p (c f) -> p c f", c=3)
                v["wo"] = M.weights[:, 3 * 2 * DFF:3 * 2 * DFF + 10 * D].rearrange("p (c f) -> p c f", c=10)
                v["OT"] = M.mixed[:, :].rearrange("p (c n) -> p c n", c=10)
                v["gate"] = M.probs[:, 0, :, :]
                return v
            if s.kind == "att" and p["big"]:
                nk = 2 if p["cross"] else 3
                v["wv"] = M.weights[:, 0:nk * 1280].rearrange("p (c f) -> p c f", c=nk)
                v["wo"] = M.weights[:, 3 * 1280:3 * 1280 + 10 * D].rearrange("p (c f) -> p c f", c=10)
                slot = [M.probs[:, 0, :, :], M.probs[:, 1, :, :]]
                slot += [M.heads[:, a:a + TB * N].rearrange("p (k n) -> p k n", k=TB) for a in (0, TB * N)]
                v["probs"] = slot
                v["psum"] = M.heads[:, 4096:6144].rearrange("p (s n) -> p s n", s=4)
                v["QT"] = M.heads[:, 6144:7168].rearrange("p (s n) -> p s n", s=2)
                v["KT"] = M.heads[:, 7168:8192].rearrange("p (s n) -> p s n", s=2)
                v["QB"] = M.heads[:, 8192:8704].bitcast(BF16).rearrange("p (s n) -> p s n", s=2)
                v["KB"] = M.heads[:, 8704:9216].bitcast(BF16).rearrange("p (s n) -> p s n", s=2)
                v["wqk"] = M.heads[:, 9216:9216 + 2 * (3 + nk) * P].rearrange("p (s c f) -> p s c f", s=2, c=3 + nk)
                v["V"] = M.values[:, 0:5120].rearrange("p (t h d) -> p t h d", t=TB, h=HEADS)
                v["OT"] = M.mixed[:, :].rearrange("p (c n) -> p c n", c=10)
                return v
            nk = 2 if p["cross"] else 3
            v["wo"] = M.weights[:, 3 * 1280:3 * 1280 + 3 * D].rearrange("p (c f) -> p c f", c=3)
            v["OT"] = M.mixed[:, 0:1536].rearrange("p (c n) -> p c n", c=3)
            v["On"] = M.mixed[:, 1536:2816].rearrange("p (t f) -> p t f", t=TB)
            if s.kind == "gated":
                return v
            v["wv"] = M.weights[:, 0:nk * D].rearrange("p (c f) -> p c f", c=nk)
            v["wq"] = M.weights[:, 960:1920].rearrange("p (c f) -> p c f", c=3)
            v["wk"] = M.weights[:, 1920:1920 + nk * D].rearrange("p (c f) -> p c f", c=nk)
            v["QS"] = M.heads[:, 0:5120].bitcast(BF16).rearrange("p (h n) -> p h n", h=HEADS)
            v["KS"] = M.heads[:, 5120:10240].bitcast(BF16).rearrange("p (h n) -> p h n", h=HEADS)
            slot = [M.probs[:, 0, :, :], M.probs[:, 1, :, :]]
            slot += [M.weights[:, a:a + TB * N].rearrange("p (k n) -> p k n", k=TB) for a in (4800, 6848, 8896)]
            slot += [M.mixed[:, 2816:2816 + TB * N].rearrange("p (k n) -> p k n", k=TB)]
            v["probs"] = slot
            nv = TB * HEADS * 32
            v["V"] = M.values[:, 0:nv].rearrange("p (t h d) -> p t h d", t=TB, h=HEADS)
            v["rest"] = M.values[:, nv:nv + 1024].rearrange("p (s n) -> p s n", s=2)
            v["parts"] = M.values[:, nv + 1024:nv + 2560].bitcast(BF16).rearrange("p (s k n) -> p s k n", s=2, k=3)
            return v

        V = {s.name: views(s) for s in stages}

        def kv_chunks(s):
            return CCH if s.prm["cross"] else CH

        def out_chunks(s):
            return [(P * c, P) for c in range(10)] if s.kind == "ff" or s.prm.get("big") else CH

        def load_weights(sp, s):
            start(sp, s, s.first)
            p, v, n = s.prm, V[s.name], 0
            w_in = s.w_in

            def load(dst, src):
                nonlocal n
                sp.dma_start(dst, src).then_inc(w_in, 16)
                n += 1

            def load_chunks(dst, src, chunks):
                full = len([1 for _, w in chunks if w == P])
                load(dst[:, 0:full, :], src[0:full * P, :].rearrange("(c p) f -> p c f", p=P))
                if full < len(chunks):
                    a, w = chunks[full]
                    load(dst[0:w, full, :], src[a:a + w, :])

            if p["ln"]:
                load(M.g_col[:, :], p["g"])
                load(M.b_col[:, :], p["be"])
            load(M.bo_row[:, :], p["bo"].rearrange("(a d) -> a d", a=1).broadcast_to([P, D]))
            load_chunks(v["wo"], p["wo"], out_chunks(s))
            if s.kind == "att":
                load_chunks(v["wv"], p["wv"], kv_chunks(s))
                if not p["big"]:
                    load_chunks(v["wq"], p["wq"], CH)
                    load_chunks(v["wk"], p["wk"], kv_chunks(s))
            elif s.kind == "ff":
                load_chunks(v["w1"], p["w1"], CH)
                load(M.b1_col[:, :], p["b1"])
            else:
                load_chunks(G["wq"], p["wq"], CH)
                for k in ("wk", "wkd", "wv", "wvd"):
                    load_chunks(G[k], p[k], CCH)
                load(G["wg"][:, :], p["wg"])
                for k, name in enumerate(("bg", "al", "dl")):
                    load(G["sc"][:, k:k + 1], p[name].rearrange("(a d) -> a d", a=1).broadcast_to([P, 1]))
            s.n_loads = n

        G = {}
        o = 0

        def take(name, n, pattern=None, **kw):
            nonlocal o
            ap = M.heads[:, o:o + n]
            G[name] = ap.rearrange(pattern, **kw) if pattern else ap
            o += n
        take("wq", 3 * 640, "p (c f) -> p c f", c=3)
        take("wk", 2 * 640, "p (c f) -> p c f", c=2)
        take("wkd", 2 * 640, "p (c f) -> p c f", c=2)
        take("wv", 2 * D, "p (c f) -> p c f", c=2)
        take("wvd", 2 * D, "p (c f) -> p c f", c=2)
        take("QP", 5 * N, "p (c n) -> p c n", c=5)
        take("wg", 2)
        take("sc", 4)
        take("gv", 32)
        take("ctD", 2 * P, "p (c n) -> p c n", c=2)
        take("ctA", 2 * P, "p (c n) -> p c n", c=2)
        take("wgb", 2 * P, "p (c n) -> p c n", c=2)
        o2 = 0
        for name, n, pat, kw in (("Kbd", 5 * P, "p (c k) -> p c k", dict(c=5)), ("Vbd", 5 * 64, "p (c k) -> p c k", dict(c=5)),
                                 ("S", 2 * 640, "p (s g k) -> p s g k", dict(s=2, g=40)), ("PT", 640, "p (c n) -> p c n", dict(c=5)),
                                 ("mx", 40, None, {}), ("sum", 40, None, {}), ("fac", 40, None, {})):
            ap = M.values[:, o2:o2 + n]
            G[name] = ap.rearrange(pat, **kw) if pat else ap
            o2 += n

        LN_BATCHES = sum(s.prm["ln"] for s in stages) * B

        def overall(s, b):
            return b + (s.index * B - s.first)

        def norm_dve(dve, n, batch):
            for t in range(TB):
                nc.vector.bn_stats(M.stats[:, t, :], M.x[:, batch * TB + t, :]).then_inc(stats, 1)
            hold(dve, stats, after(n, TB, TB))
            for t in range(TB):
                nc.vector.bn_aggr(M.mv[:, t, :], M.stats[:, t, :]).then_inc(mv, 1)
            dve.wait_ge(rstd, after(n, 1, 1))
            for t in range(TB):
                nc.vector.tensor_scalar(M.xn[:, t, :], M.x[:, batch * TB + t, :], M.mv[:, t, 0:1], M.rstd[:, t:t + 1],
                                        ALU.subtract, ALU.mult).then_inc(xn, 1)

        def norm_pool(pool, n):
            hold(pool, mv, after(n, TB, TB))
            nc.gpsimd.tensor_scalar(M.vare[:, :], M.mv[:, :, 1], EPS, 1.0, ALU.add, ALU.mult).then_inc(vare, 1)
            hold(pool, vare, after(n, 1, 1))
            nc.gpsimd.tensor_tensor(M.rstd[:, :], M.vare[:, :], M.mhalf[:, :], ALU.pow).then_inc(rstd, 1)

        def norm_next_dve(dve, s, b):
            if s.prm["ln"]:
                norm_dve(dve, overall(s, b) + 1, (b + 1 - s.first) % B)

        def copy_pool(batch):
            for t in range(TB):
                nc.gpsimd.tensor_copy(M.xn[:, t, :], M.x[:, batch * TB + t, :]).then_inc(xcopy, 1)

        def norm_next_pool(pool, s, b):
            if s.prm["ln"]:
                norm_pool(pool, overall(s, b) + 1)
            else:
                hold(pool, s.sem("in_ps" + s.tag), after(b - s.first, n_in(s), 3))
                copy_pool((b + 1 - s.first) % B)

        def inputs_pe(pe, s, b):
            if s.prm["ln"]:
                hold(pe, xn, after(overall(s, b), TB, TB))
            else:
                hold(pe, xcopy, after(overall(s, b) - LN_BATCHES, TB, TB))
            k = 0
            for a, w in CH:
                if k >= 2:
                    hold(pe, s.sem("in_evac" + s.tag), after(b - s.first, n_in(s), k - 1))
                for t in range(TB):
                    last = nc.tensor.transpose(M.PJ[k % 2][0:w, t * P:t * P + P], M.xn[:, t, a:a + w], M.ident[:, :])
                last.then_inc(s.sem("in_ps" + s.tag), 1)
                k += 1
            if s.prm["cross"]:
                pe.wait_ge(s.sem("ctx_in" + s.tag), after(b - s.first, 16, 16))
                for a, w in CCH:
                    hold(pe, s.sem("in_evac" + s.tag), after(b - s.first, n_in(s), k - 1))
                    for t in range(TB):
                        last = nc.tensor.transpose(M.PJ[k % 2][0:w, t * P:t * P + P], M.ctx_in[:, t, a:a + w], M.ident[:, :])
                    last.then_inc(s.sem("in_ps" + s.tag), 1)
                    k += 1

        def n_in(s):
            return 5 if s.prm["cross"] else 3

        def inputs_act(act, s, b):
            k = 0
            for c, (a, w) in enumerate(CH):
                act.wait_ge(s.sem("in_ps" + s.tag), after(b - s.first, n_in(s), k + 1))
                if s.prm["ln"]:
                    if c == 0:
                        act.wait_ge(s.w_in, 16 * s.n_loads)
                    ins = nc.scalar.activation(M.hT[0:w, c, :], M.PJ[k % 2][0:w, :], ACT.Identity,
                                               bias=M.b_col[0:w, c:c + 1], scale=M.g_col[0:w, c:c + 1])
                else:
                    ins = nc.scalar.copy(M.hT[0:w, c, :], M.PJ[k % 2][0:w, :])
                ins.then_inc(s.sem("in_evac" + s.tag), 1)
                k += 1
            if s.prm["cross"]:
                for c, (a, w) in enumerate(CCH):
                    act.wait_ge(s.sem("in_ps" + s.tag), after(b - s.first, n_in(s), k + 1))
                    nc.scalar.copy(M.cT[0:w, c, :], M.PJ[k % 2][0:w, :]).then_inc(s.sem("in_evac" + s.tag), 1)
                    k += 1

        def kvT(s):
            return M.cT if s.prm["cross"] else M.hT

        def out_pe(pe, s, b):
            v, chunks = V[s.name], out_chunks(s)
            nch = len(chunks)
            if s.kind == "gated" or not s.prm.get("big", True):
                for c, (a, w) in enumerate(chunks):
                    if c >= 2:
                        hold(pe, s.sem("ot"), after(b, nch, c - 1))
                    for t in range(TB):
                        last = nc.tensor.transpose(M.PJ[c % 2][0:w, t * P:t * P + P], v["On"][:, t, a:a + w], M.ident[:, :])
                    last.then_inc(s.sem("ot_ps"), 1)
            if not s.prm.get("big"):
                pe.wait_ge(s.sem("ot"), after(b, nch, nch))
            for t in range(TB):
                if t >= 2:
                    pe.wait_ge(x_done, after(b, TB, (s.index * B - s.first) * TB + X_IN + t - 1))
                for c, (a, w) in enumerate(chunks):
                    if s.prm.get("big") and t == 0 and c in (nch - 2, nch - 1):
                        pe.wait_ge(s.sem("on"), seeded(b, PAIRS, PAIRS if c == nch - 1 else PAIRS - 1))
                    last = nc.tensor.matmul(M.SM[t % 2][:, 0:D], v["OT"][0:w, c, t * P:t * P + P], v["wo"][0:w, c, :],
                                            start=c == 0, stop=c == nch - 1)
                last.then_inc(s.sem("y"), 1)

        def out_act(act, s, b):
            v, chunks = V[s.name], out_chunks(s)
            for c, (a, w) in enumerate(chunks):
                act.wait_ge(s.sem("ot_ps"), after(b, len(chunks), c + 1))
                nc.scalar.copy(v["OT"][0:w, c, :], M.PJ[c % 2][0:w, :]).then_inc(s.sem("ot"), 1)

        def out_dve(dve, s, b):
            for t in range(TB):
                dve.wait_ge(s.sem("y"), after(b, TB, t + 1))
                nc.vector.tensor_tensor(M.ysum[:, t % 2, :], M.SM[t % 2][:, 0:D], M.bo_row[:, :], ALU.add).then_inc(s.sem("ysum"), 1)
                dve.wait_ge(s.sem("ysum"), after(b, TB, t + 1))
                nc.vector.tensor_tensor(M.x[:, (b - s.first) * TB + t, :], M.ysum[:, t % 2, :], M.x[:, (b - s.first) * TB + t, :],
                                        ALU.add).then_inc(x_done, 1)

        def v_slices(s):
            return [(0, 8), (8, 8), (16, 4)] if s.prm["big"] else [(0, 20)]

        def values_pe(pe, s, b, t):
            v, dh, sl, kv = V[s.name], s.prm["dh"], v_slices(s), kv_chunks(s)
            if t == 0:
                pe.wait_ge(s.w_in, 16 * s.n_loads)
                hold(pe, s.sem("in_evac" + s.tag), after(b - s.first, n_in(s), n_in(s)))
            for j, (h0, nh) in enumerate(sl):
                k = t * len(sl) + j
                if k >= 2:
                    pe.wait_ge(s.sem("v"), after(b, TB * len(sl), k - 1))
                for c, (a, w) in enumerate(kv):
                    last = nc.tensor.matmul(M.PJ[k % 2][:, 0:nh * dh], kvT(s)[0:w, c, t * P:t * P + P],
                                            v["wv"][0:w, c, h0 * dh:(h0 + nh) * dh], start=c == 0, stop=c == len(kv) - 1)
                last.then_inc(s.sem("v_ps"), 1)

        def values_act(act, s, b):
            v, dh, sl = V[s.name], s.prm["dh"], v_slices(s)
            k = 0
            for t in range(TB):
                for h0, nh in sl:
                    act.wait_ge(s.sem("v_ps"), after(b, TB * len(sl), k + 1))
                    nc.scalar.copy(v["V"][:, t, h0:h0 + nh, 0:dh],
                                   M.PJ[k % 2][:, 0:nh * dh].rearrange("p (h d) -> p h d", h=nh)).then_inc(s.sem("v"), 1)
                    k += 1

        def stack_pe(pe, s, b):
            v = V[s.name]
            pe.wait_ge(s.w_in, 16 * s.n_loads)
            hold(pe, s.sem("in_evac" + s.tag), after(b - s.first, n_in(s), n_in(s)))
            for k in range(6):
                c, (a, w) = k // 2, CH[k // 2]
                if k == 4:
                    hold(pe, s.sem("rest"), after(b, 6, 4))
                    for t in range(TB):
                        values_pe(pe, s, b, t)
                    hold(pe, s.sem("v"), after(b, TB, TB))
                elif k >= 2:
                    pe.wait_ge(s.sem("rest"), after(b, 6, k - 1))
                wt, src, ch = (v["wq"], M.hT, CH) if k % 2 == 0 else (v["wk"], kvT(s), kv_chunks(s))
                for e, (_, ew) in enumerate(ch):
                    last = nc.tensor.matmul(M.PJ[k % 2][0:w, :], wt[0:ew, e, a:a + w], src[0:ew, e, :], start=e == 0, stop=e == len(ch) - 1)
                last.then_inc(s.sem("qk_ps"), 1)

        def stack_act(act, s, b):
            v = V[s.name]
            for k in range(6):
                w = CH[k // 2][1]
                if k == 4:
                    values_act(act, s, b)
                act.wait_ge(s.sem("qk_ps"), after(b, 6, k + 1))
                if k >= 2:
                    act.wait_ge(s.sem(f"stack{k % 2}"), after(b, 3 * 96, 96 * (k // 2)))
                nc.scalar.copy(v["parts"][0:w, k % 2, 0, :], M.PJ[k % 2][0:w, :]).then_inc(s.sem("hi"), 1)

        def stack_dve(dve, s, b, ks):
            v = V[s.name]
            for k in ks:
                w = CH[k // 2][1]
                dve.wait_ge(s.sem("hi"), after(b, 6, k + 1))
                if k >= 2:
                    dve.wait_ge(s.sem("lo"), after(b, 6, k - 1))
                nc.vector.tensor_tensor(v["rest"][0:w, k % 2, :], M.PJ[k % 2][0:w, :], v["parts"][0:w, k % 2, 0, :],
                                        ALU.subtract).then_inc(s.sem("rest"), 1)

        def stack_pool(pool, s, b):
            v = V[s.name]
            for k in range(6):
                w = CH[k // 2][1]
                hold(pool, s.sem("rest"), after(b, 6, k + 1))
                if k >= 2:
                    hold(pool, s.sem(f"stack{k % 2}"), after(b, 3 * 96, 96 * (k // 2)))
                nc.gpsimd.tensor_copy(v["parts"][0:w, k % 2, 1, :], v["rest"][0:w, k % 2, :]).then_inc(s.sem("mid"), 1)
                hold(pool, s.sem("mid"), after(b, 6, k + 1))
                nc.gpsimd.tensor_tensor(v["parts"][0:w, k % 2, 2, :], v["rest"][0:w, k % 2, :], v["parts"][0:w, k % 2, 1, :],
                                        ALU.subtract).then_inc(s.sem("lo"), 1)

        def stack_sync(sp, s, b):
            v = V[s.name]
            for k in range(6):
                c, (a, w) = k // 2, CH[k // 2]
                nh = w // 16
                dst, order = (v["QS"], Q_PARTS) if k % 2 == 0 else (v["KS"], K_PARTS)
                sp.wait_ge(s.sem("lo"), after(b, 6, k + 1))
                for j, part in enumerate(order):
                    sp.dma_start(dst[16 * j:16 * j + 16, 8 * c:8 * c + nh, :],
                                 v["parts"][0:w, k % 2, "hml".index(part), :]).then_inc(s.sem(f"stack{k % 2}"), 16)

        PAIRS = HEADS // 2

        def slot_loads(u):
            return u // 2

        def project_pe(pe, s, b, u, which):
            v = V[s.name]
            ch = CH if which == "q" else kv_chunks(s)
            src = M.hT if which == "q" else kvT(s)
            bank, off = (M.PJ[0], 0) if which == "q" else (M.PJ[1], 3)
            if which == "q":
                pe.wait_ge(s.sem(f"wqk{u % 2}"), after(b, 16 * PAIRS // 2, 16 * (slot_loads(u) + 1)))
            pe.wait_ge(s.sem(which + "_evac"), seeded(b, PAIRS, u))
            for e, (_, ew) in enumerate(ch):
                last = nc.tensor.matmul(bank[:, :], v["wqk"][0:ew, u % 2, off + e, :], src[0:ew, e, :], start=e == 0, stop=e == len(ch) - 1)
            last.then_inc(s.sem(which + "_ps"), 1)

        def project_act(act, s, b, u, which):
            v = V[s.name]
            act.wait_ge(s.sem(which + "_ps"), seeded(b, PAIRS, u + 1))
            act.wait_ge(s.sem("st"), seeded(b, UNITS, 8 * (u - 1)))
            bank = M.PJ[0] if which == "q" else M.PJ[1]
            nc.scalar.copy(v["QT" if which == "q" else "KT"][:, u % 2, :], bank[:, :])
            nc.scalar.copy(v["QB" if which == "q" else "KB"][:, u % 2, :], bank[:, :]).then_inc(s.sem(which + "_evac"), 1)

        def rows_pe(pe, s, b, u, t):
            v = V[s.name]
            g, qb = t // TB, t % TB
            if t == 0:
                pe.wait_ge(s.sem("q_evac"), seeded(b, PAIRS, u + 1))
                pe.wait_ge(s.sem("k_evac"), seeded(b, PAIRS, u + 1))
            pe.wait_ge(s.sem("max"), seeded(b, UNITS, 8 * u + t - 1))
            strip = slice(64 * g, 64 * g + 64)
            nc.tensor.matmul(M.SM[t % 2][:, :], v["QB"][strip, u % 2, qb * P:qb * P + P], v["KB"][strip, u % 2, :],
                             start=True, stop=True).then_inc(s.sem("rows"), 1)

        def max_dve(dve, s, b, u, t, group, slots):
            if t == 0:
                dve.wait_ge(s.sem("nm_ps"), seeded(b, UNITS // group, u - slots + 1))
            dve.wait_ge(s.sem("rows"), seeded(b, UNITS, group * u + t + 1))
            nc.vector.tensor_reduce(M.negm[:, u % slots, t % TB, t // TB:t // TB + 1], M.SM[t % 2][:, :], AX.X, ALU.max,
                                    negate=True).then_inc(s.sem("max"), 1)

        def negm_pe(pe, s, b, u):
            pe.wait_ge(s.sem("max"), seeded(b, UNITS, 8 * u + 8))
            for qb in range(TB):
                last = nc.tensor.transpose(M.SM[0][0:2, qb * P:qb * P + P], M.negm[:, u % 2, qb, 0:2], M.ident[:, :])
            last.then_inc(s.sem("nm_ps"), 1)

        def negm_act(act, s, b, u):
            act.wait_ge(s.sem("nm_ps"), seeded(b, PAIRS, u + 1))
            act.wait_ge(s.sem("st"), seeded(b, UNITS, 8 * (u - 1)))
            for g in range(2):
                last = nc.scalar.copy(M.nmT[64 * g:64 * g + 2, u % 2, :], M.SM[0][0:2, :])
            last.then_inc(s.sem("nm_hi"), 1)

        def negm_dve(dve, s, b, u):
            dve.wait_ge(s.sem("nm_hi"), seeded(b, PAIRS, u + 1))
            for g in range(2):
                last = nc.vector.tensor_tensor(M.nmT[64 * g + 32:64 * g + 34, u % 2, :], M.SM[0][0:2, :], M.nmT[0:2, u % 2, :], ALU.subtract)
            last.then_inc(s.sem("nm_lo"), 1)

        def columns_pe(pe, s, b, u, t):
            v = V[s.name]
            g, kb = t // TB, t % TB
            pe.wait_ge(s.sem("exp"), seeded(b, UNITS, 8 * u + t - 1))
            strip, mstrip = slice(64 * g, 64 * g + 64), slice(64 * g, 64 * g + 34)
            nc.tensor.matmul(M.ST[t % 2][:, :], v["KT"][strip, u % 2, kb * P:kb * P + P], v["QT"][strip, u % 2, :], start=True, stop=False)
            if t == 0:
                pe.wait_ge(s.sem("nm_lo"), seeded(b, PAIRS, u + 1))
            nc.tensor.matmul(M.ST[t % 2][:, :], M.sel[mstrip, :], M.nmT[mstrip, u % 2, :], start=False, stop=True).then_inc(s.sem("st"), 1)

        def exp_act(act, s, b, k):
            v, h, kb = V[s.name], k // TB, k % TB
            slots = len(v["probs"])
            act.wait_ge(s.sem("st"), seeded(b, UNITS, k + 1))
            if kb == 0:
                act.wait_ge(s.sem("av"), seeded(b, HEADS // s.prm["group"], (h - slots) // s.prm["group"] + 1))
                if s.prm["big"]:
                    act.wait_ge(s.sem("psum"), seeded(b, HEADS, h - slots + 1))
            nc.scalar.activation(v["probs"][h % slots][:, kb, :], M.ST[k % 2][:, :], ACT.Exp,
                                 scale=float(s.prm["dh"]) ** -0.5).then_inc(s.sem("exp"), 1)

        def mix_pe(pe, s, b, u, kb):
            v, n = V[s.name], s.prm["group"]
            w = P // n
            if kb == 0:
                pe.wait_ge(s.sem("exp"), seeded(b, UNITS, n * TB * (u + 1)))
                pe.wait_ge(s.sem("ob"), seeded(b, HEADS // n, u))
            for g in range(n):
                h = n * u + g
                last = nc.tensor.matmul(M.OB[w * g:w * g + w, :], v["V"][:, kb, h, :], v["probs"][h % len(v["probs"])][:, kb, :],
                                        start=kb == 0, stop=kb == TB - 1)
            if kb == TB - 1:
                last.then_inc(s.sem("av"), 1)

        def psum_dve(dve, s, b, h, j):
            v, c = V[s.name], slice(j * P, j * P + P)
            if j == 0:
                dve.wait_ge(s.sem("exp"), seeded(b, UNITS, TB * (h + 1)))
                dve.wait_ge(s.sem("den"), seeded(b, PAIRS, (h - 4) // 2 + 1))
            last = nc.vector.tensor_reduce(v["psum"][:, h % 4, c], v["probs"][h % 4][:, :, c].rearrange("p k n -> p n k"), AX.X, ALU.add)
            if j == TB - 1:
                last.then_inc(s.sem("psum"), 1)

        def sums_pe(pe, s, b, u):
            v = V[s.name]
            pe.wait_ge(s.sem("psum"), seeded(b, HEADS, 2 * u + 2))
            pe.wait_ge(s.sem("rcp"), seeded(b, 4 * PAIRS, 4 * u))
            for g in range(2):
                last = nc.tensor.matmul(M.TR[64 * g:64 * g + 64, :], M.ones[:, :], v["psum"][:, (2 * u + g) % 4, :], start=True, stop=True)
            last.then_inc(s.sem("den"), 1)

        def recip_dve(dve, s, b, u, j):
            c = slice(j * P, j * P + P)
            if j == 0:
                dve.wait_ge(s.sem("den"), seeded(b, PAIRS, u + 1))
            nc.vector.reciprocal(M.rec[:, c], M.TR[:, c]).then_inc(s.sem("rcp"), 1)

        def divide_dve(dve, s, b, u):
            v = V[s.name]
            dve.wait_ge(s.sem("rcp"), seeded(b, 4 * PAIRS, 4 * u + 4))
            dve.wait_ge(s.sem("ob"), seeded(b, PAIRS, u + 1))
            nc.vector.tensor_tensor(v["OT"][:, u, :], v["OT"][:, u, :], M.rec[:, :], ALU.mult).then_inc(s.sem("on"), 1)

        def evac_act(act, s, b, u):
            v, n = V[s.name], s.prm["group"]
            act.wait_ge(s.sem("av"), seeded(b, HEADS // n, u + 1))
            if s.prm["big"]:
                nc.scalar.copy(v["OT"][:, u, :], M.OB[:, :]).then_inc(s.sem("ob"), 1)
            else:
                act.wait_ge(s.sem("ox_ps"), seeded(b, HEADS // n, u))
                nc.scalar.copy(M.ox[:, :], M.OB[:, :]).then_inc(s.sem("ob"), 1)

        def wide_pe(pe, s, b):
            project_pe(pe, s, b, 0, "q")
            project_pe(pe, s, b, 0, "k")
            for t in range(8):
                rows_pe(pe, s, b, 0, t)
            for u in range(PAIRS):
                more = u + 1 < PAIRS
                if more:
                    project_pe(pe, s, b, u + 1, "q")
                negm_pe(pe, s, b, u)
                if more:
                    project_pe(pe, s, b, u + 1, "k")
                for t in range(8):
                    columns_pe(pe, s, b, u, t)
                    if more:
                        rows_pe(pe, s, b, u + 1, t)
                    if u and t < TB:
                        mix_pe(pe, s, b, u - 1, t)
                    if u and t == TB:
                        sums_pe(pe, s, b, u - 1)
            for kb in range(TB):
                mix_pe(pe, s, b, PAIRS - 1, kb)
            sums_pe(pe, s, b, PAIRS - 1)

        def wide_act(act, s, b):
            project_act(act, s, b, 0, "q")
            project_act(act, s, b, 0, "k")
            for u in range(PAIRS):
                more = u + 1 < PAIRS
                if more:
                    project_act(act, s, b, u + 1, "q")
                negm_act(act, s, b, u)
                if more:
                    project_act(act, s, b, u + 1, "k")
                for t in range(8):
                    exp_act(act, s, b, 8 * u + t)
                    if u and t == TB:
                        evac_act(act, s, b, u - 1)
            evac_act(act, s, b, PAIRS - 1)

        def wide_dve(dve, s, b):
            for t in range(8):
                max_dve(dve, s, b, 0, t, 8, 2)
            for u in range(PAIRS):
                negm_dve(dve, s, b, u)
                if u > 1:
                    recip_dve(dve, s, b, u - 2, 3)
                    divide_dve(dve, s, b, u - 2)
                for t in range(8):
                    if u + 1 < PAIRS:
                        max_dve(dve, s, b, u + 1, t, 8, 2)
                    if t >= TB:
                        psum_dve(dve, s, b, 2 * u, t - TB)
                    elif u:
                        psum_dve(dve, s, b, 2 * u - 1, t)
                    if u and t > TB:
                        recip_dve(dve, s, b, u - 1, t - TB - 1)
            recip_dve(dve, s, b, PAIRS - 2, 3)
            divide_dve(dve, s, b, PAIRS - 2)
            for j in range(TB):
                psum_dve(dve, s, b, HEADS - 1, j)
            for j in range(TB):
                recip_dve(dve, s, b, PAIRS - 1, j)
            divide_dve(dve, s, b, PAIRS - 1)

        FOURS = HEADS // 4

        def rows4_pe(pe, s, b, u, t):
            v = V[s.name]
            h, qb = 4 * u + t // TB, t % TB
            if t == 0 and u % 2 == 0:
                for k in range(2):
                    hold(pe, s.sem(f"stack{k}"), after(b, 3 * 96, 96 * (u // 2 + 1)))
            pe.wait_ge(s.sem("max"), seeded(b, UNITS, 16 * u + t - 1))
            nc.tensor.matmul(M.SM[t % 2][:, :], v["QS"][0:96, h, qb * P:qb * P + P], v["KS"][0:96, h, :],
                             start=True, stop=True).then_inc(s.sem("rows"), 1)

        def negm4_pe(pe, s, b, u):
            pe.wait_ge(s.sem("max"), seeded(b, UNITS, 16 * u + 16))
            pe.wait_ge(s.sem("nm_lo"), seeded(b, FOURS, u))
            for qb in range(TB):
                last = nc.tensor.transpose(M.TR[0:4, qb * P:qb * P + P], M.negm[:, u % 3, qb, :], M.ident[:, :])
            last.then_inc(s.sem("nm_ps"), 1)

        def negm4_act(act, s, b, u):
            act.wait_ge(s.sem("nm_ps"), seeded(b, FOURS, u + 1))
            if u >= 2:
                act.wait_ge(s.sem(f"nm{u % 2}"), after(b, 32 * (3 - u % 2), 32 * (u // 2)))
            nc.scalar.copy(M.nmT[0:4, u % 2, :], M.TR[0:4, :]).then_inc(s.sem("nm_hi"), 1)

        def negm4_dve(dve, s, b, u):
            dve.wait_ge(s.sem("nm_hi"), seeded(b, FOURS, u + 1))
            nc.vector.tensor_tensor(M.nmT[32:36, u % 2, :], M.TR[0:4, :], M.nmT[0:4, u % 2, :], ALU.subtract).then_inc(s.sem("nm_lo"), 1)

        def negm4_sync(sp, s, b, u):
            v = V[s.name]
            sp.wait_ge(s.sem("nm_lo"), seeded(b, FOURS, u + 1))
            for row, part in ((96, 0), (97, 32)):
                sp.dma_start(v["QS"][row:row + 1, 4 * u:4 * u + 4, :], M.nmT[part:part + 4, u % 2, :]).then_inc(s.sem(f"nm{u % 2}"), 16)

        def columns4_pe(pe, s, b, u, t):
            v = V[s.name]
            h, kb = 4 * u + t // TB, t % TB
            if t == 0:
                pe.wait_ge(s.sem(f"nm{u % 2}"), after(b, 32 * (3 - u % 2), 32 * (u // 2 + 1)))
            pe.wait_ge(s.sem("exp"), seeded(b, UNITS, 16 * u + t - 1))
            nc.tensor.matmul(M.ST[t % 2][:, :], v["KS"][0:98, h, kb * P:kb * P + P], v["QS"][0:98, h, :],
                             start=True, stop=True).then_inc(s.sem("st"), 1)

        def turn4_pe(pe, s, b, u):
            pe.wait_ge(s.sem("ob"), seeded(b, FOURS, u + 1))
            pe.wait_ge(s.sem("on"), seeded(b, FOURS, u))
            for t in range(TB):
                last = nc.tensor.transpose(M.PJ[0][:, t * P:t * P + P], M.ox[:, t * P:t * P + P], M.ident[:, :])
            last.then_inc(s.sem("ox_ps"), 1)

        def divide4_dve(dve, s, b, u):
            v = V[s.name]
            out = M.PJ[0][:, :].rearrange("p (t g d) -> p t g d", t=TB, g=4)
            rec = M.rec[:, 0:16].rearrange("p (t g) -> p t g", t=TB)
            dve.wait_ge(s.sem("ox_ps"), seeded(b, FOURS, u + 1))
            nc.vector.reciprocal(rec, out[:, :, :, 16]).then_inc(s.sem("rcp"), 1)
            dve.wait_ge(s.sem("rcp"), seeded(b, FOURS, u + 1))
            nc.vector.tensor_tensor(v["On"][:, :, 64 * u:64 * u + 64].rearrange("p t (g d) -> p t g d", g=4), out[:, :, :, 0:16],
                                    rec.unsqueeze(3).broadcast_to([P, TB, 4, 16]), ALU.mult).then_inc(s.sem("on"), 1)

        def narrow_pe(pe, s, b):
            for t in range(16):
                rows4_pe(pe, s, b, 0, t)
            for t in range(16):
                rows4_pe(pe, s, b, 1, t)
                if t == 1:
                    negm4_pe(pe, s, b, 0)
            for u in range(FOURS):
                for t in range(16):
                    columns4_pe(pe, s, b, u, t)
                    if t == 2 and u + 1 < FOURS:
                        negm4_pe(pe, s, b, u + 1)
                    if u + 2 < FOURS:
                        rows4_pe(pe, s, b, u + 2, t)
                    if u and t in (1, 3, 5, 7):
                        mix_pe(pe, s, b, u - 1, t // 2)
                    if u and t == 11:
                        turn4_pe(pe, s, b, u - 1)
            for kb in range(TB):
                mix_pe(pe, s, b, FOURS - 1, kb)
            turn4_pe(pe, s, b, FOURS - 1)
            hold(pe, s.sem("on"), seeded(b, FOURS, FOURS))

        def narrow_act(act, s, b):
            negm4_act(act, s, b, 0)
            for u in range(FOURS):
                for t in range(16):
                    exp_act(act, s, b, 16 * u + t)
                    if t == 2 and u + 1 < FOURS:
                        negm4_act(act, s, b, u + 1)
                    if u and t == 8:
                        evac_act(act, s, b, u - 1)
            evac_act(act, s, b, FOURS - 1)

        def narrow_dve(dve, s, b):
            for t in range(16):
                max_dve(dve, s, b, 0, t, 16, 3)
                if t in (8, 12):
                    stack_dve(dve, s, b, [t // 4 + 2])
            for t in range(16):
                max_dve(dve, s, b, 1, t, 16, 3)
                if t == 2:
                    negm4_dve(dve, s, b, 0)
            for u in range(FOURS):
                for t in range(16):
                    if u + 2 < FOURS:
                        max_dve(dve, s, b, u + 2, t, 16, 3)
                    if t == 3 and u + 1 < FOURS:
                        negm4_dve(dve, s, b, u + 1)
                    if u and t == 13:
                        divide4_dve(dve, s, b, u - 1)
            divide4_dve(dve, s, b, FOURS - 1)

        def attention_pe(pe, s):
            with pe.Fori(s.first, s.first + B) as b:
                inputs_pe(pe, s, b)
                start(pe, s, b)
                if s.prm["big"]:
                    for t in range(TB):
                        values_pe(pe, s, b, t)
                    hold(pe, s.sem("v"), after(b, 3 * TB, 3 * TB))
                    wide_pe(pe, s, b)
                else:
                    stack_pe(pe, s, b)
                    narrow_pe(pe, s, b)
                out_pe(pe, s, b)

        def attention_act(act, s):
            with act.Fori(s.first, s.first + B) as b:
                inputs_act(act, s, b)
                start(act, s, b)
                if s.prm["big"]:
                    values_act(act, s, b)
                    wide_act(act, s, b)
                else:
                    stack_act(act, s, b)
                    narrow_act(act, s, b)
                    out_act(act, s, b)

        def attention_dve(dve, s):
            start(dve, s, s.first)
            v = V[s.name]
            if not s.prm["big"]:
                nc.vector.memset(v["V"][:, :, :, 16:32], 1.0)
                nc.vector.memset(v["KS"][96:98, :, :], 1.0)
            with dve.Fori(s.first, s.first + B) as b:
                start(dve, s, b)
                if s.prm["big"]:
                    wide_dve(dve, s, b)
                else:
                    stack_dve(dve, s, b, range(4))
                    narrow_dve(dve, s, b)
                dve.wait_ge(s.w_in, 16 * s.n_loads)
                norm_next_dve(dve, s, b)
                out_dve(dve, s, b)

        def attention_pool(pool, s):
            with pool.Fori(s.first, s.first + B) as b:
                start(pool, s, b)
                if s.kind == "att" and not s.prm["big"]:
                    stack_pool(pool, s, b)
                norm_next_pool(pool, s, b)

        def load_context(sp, s, b):
            sp.dma_start(M.ctx_in[:, :, :], io["ctx"][bass.ts(b - s.first, N), :].rearrange("(t p) d -> p t d", p=P)
                         ).then_inc(s.sem("ctx_in" + s.tag), 16)

        def attention_sync(sp, s):
            load_weights(sp, s)
            with sp.Fori(s.first, s.first + B) as b:
                start(sp, s, b)
                if s.prm["cross"]:
                    load_context(sp, s, b)
                if s.prm["big"]:
                    for u in range(PAIRS):
                        sp.wait_ge(s.sem("k_ps"), seeded(b, PAIRS, u - 1))
                        sp.dma_start(V[s.name]["wqk"][:, u % 2, :, :],
                                     s.prm["wqk"][u * P:u * P + P, :].rearrange("p (c f) -> p c f", f=P)).then_inc(s.sem(f"wqk{u % 2}"), 16)
                else:
                    stack_sync(sp, s, b)
                    for u in range(FOURS):
                        negm4_sync(sp, s, b, u)

        NF = DFF // P

        def ff_pe(pe, s):
            v = V[s.name]
            with pe.Fori(s.first, s.first + B) as b:
                inputs_pe(pe, s, b)
                start(pe, s, b)
                pe.wait_ge(s.w_in, 16 * s.n_loads)
                hold(pe, s.sem("in_evac" + s.tag), after(b - s.first, 3, 3))
                for j in range(NF):
                    if j >= 2:
                        pe.wait_ge(s.sem("ot"), after(b, NF, j - 1))
                    for half, bank in ((1, M.ST[j % 2]), (0, M.PJ[j % 2])):
                        for e, (_, w) in enumerate(CH):
                            last = nc.tensor.matmul(bank[:, :], v["w1"][0:w, e, half * DFF + j * P:half * DFF + j * P + P],
                                                    M.hT[0:w, e, :], start=e == 0, stop=e == 2)
                        last.then_inc(s.sem("a_ps" if half == 0 else "g_ps"), 1)
                out_pe(pe, s, b)

        def ff_act(act, s):
            v = V[s.name]
            with act.Fori(s.first, s.first + B) as b:
                inputs_act(act, s, b)
                start(act, s, b)
                for j in range(NF):
                    act.wait_ge(s.sem("g_ps"), after(b, NF, j + 1))
                    if j >= 2:
                        act.wait_ge(s.sem("ot"), after(b, NF, j - 1))
                    nc.scalar.activation(v["gate"][:, j % 2, :], M.ST[j % 2][:, :], s.prm["gelu"],
                                         bias=M.b1_col[:, NF + j:NF + j + 1]).then_inc(s.sem("gelu"), 1)

        def ff_dve(dve, s):
            v = V[s.name]
            with dve.Fori(s.first, s.first + B) as b:
                start(dve, s, b)
                dve.wait_ge(s.w_in, 16 * s.n_loads)
                for j in range(NF):
                    dve.wait_ge(s.sem("gelu"), after(b, NF, j + 1))
                    dve.wait_ge(s.sem("a_ps"), after(b, NF, j + 1))
                    nc.vector.scalar_tensor_tensor(out=v["OT"][:, j, :], in0=M.PJ[j % 2][:, :], scalar=M.b1_col[:, j:j + 1],
                                                   in1=v["gate"][:, j % 2, :], op0=ALU.add, op1=ALU.mult).then_inc(s.sem("ot"), 1)
                norm_next_dve(dve, s, b)
                out_dve(dve, s, b)

        def gated_pe(pe, s):
            v = V[s.name]
            A, Bk = M.ST[0], M.ST[1]
            with pe.Fori(s.first, s.first + B) as b:
                inputs_pe(pe, s, b)
                start(pe, s, b)
                pe.wait_ge(s.w_in, 16 * s.n_loads)
                hold(pe, s.sem("in_evac" + s.tag), after(b - s.first, 5, 5))
                for c in range(5):
                    if c >= 2:
                        pe.wait_ge(s.sem("qp"), after(b, 5, c - 1))
                    for e, (_, w) in enumerate(CH):
                        last = nc.tensor.matmul(M.PJ[c % 2][:, :], G["wq"][0:w, e, c * P:c * P + P], M.hT[0:w, e, :], start=e == 0, stop=e == 2)
                    last.then_inc(s.sem("qp_ps"), 1)
                pe.wait_ge(s.sem("tok"), after(b, 4, 4))
                for c in range(5):
                    for e, (_, w) in enumerate(CCH):
                        nc.tensor.matmul(M.SM[0][:, c * 32:c * 32 + 32], G["wkd"][0:w, e, c * P:c * P + P], G["ctD"][0:w, e, 0:32],
                                         start=e == 0, stop=False)
                    for e, (_, w) in enumerate(CCH):
                        last = nc.tensor.matmul(M.SM[0][:, c * 32:c * 32 + 32], G["wk"][0:w, e, c * P:c * P + P], G["ctA"][0:w, e, 0:32],
                                                start=False, stop=e == 1)
                for e, (_, w) in enumerate(CCH):
                    last = nc.tensor.matmul(M.SM[0][:, 256:256 + NTOK], G["wgb"][0:w, e, :], G["ctD"][0:w, e, 0:NTOK],
                                            start=e == 0, stop=e == 1)
                last.then_inc(s.sem("k_ps"), 1)
                for src, wt, first in (("ctD", "wvd", True), ("ctA", "wv", False)):
                    for e, (_, w) in enumerate(CCH):
                        last = nc.tensor.matmul(M.SM[1][:, 0:D], G[src][0:w, e, :], G[wt][0:w, e, :],
                                                start=first and e == 0, stop=(not first) and e == 1)
                last.then_inc(s.sem("v_ps"), 1)
                pe.wait_ge(s.sem("qp"), after(b, 5, 5))
                pe.wait_ge(s.sem("kbd"), after(b, 4, 4))
                pe.wait_ge(s.sem("vbd"), after(b, 4, 4))
                def scores(qb):
                    if qb:
                        pe.wait_ge(s.sem("sub"), after(b, 2 * TB, 2 * qb))
                    for c in range(5):
                        last = nc.tensor.matmul((A if c < 4 else Bk)[:, (c % 4) * P:(c % 4) * P + P], G["QP"][:, c, qb * P:qb * P + P],
                                                G["Kbd"][:, c, :], start=True, stop=True)
                    last.then_inc(s.sem("s_ps"), 1)

                scores(0)
                for qb in range(TB):
                    if qb + 1 < TB:
                        scores(qb + 1)
                    pe.wait_ge(s.sem("p"), after(b, TB, qb + 1))
                    for c in range(5):
                        last = nc.tensor.transpose((M.PJ[0] if c < 4 else M.PJ[1])[:, (c % 4) * P:(c % 4) * P + P],
                                                   G["S"][:, qb % 2, 8 * c:8 * c + 8, :], M.ident[:, :])
                    last.then_inc(s.sem("pt_ps"), 1)
                    pe.wait_ge(s.sem("pt"), after(b, 2 * TB, 2 * qb + 2))
                    if qb:
                        pe.wait_ge(s.sem("on"), after(b, TB, qb))
                    for c in range(5):
                        last = nc.tensor.matmul(M.OB[:, c * 64:c * 64 + 64], G["PT"][:, c, :], G["Vbd"][:, c, :], start=True, stop=True)
                    last.then_inc(s.sem("o_ps"), 1)
                pe.wait_ge(s.sem("on"), after(b, TB, TB))
                out_pe(pe, s, b)

        def gated_act(act, s):
            v = V[s.name]
            with act.Fori(s.first, s.first + B) as b:
                inputs_act(act, s, b)
                start(act, s, b)
                for c in range(5):
                    act.wait_ge(s.sem("qp_ps"), after(b, 5, c + 1))
                    nc.scalar.copy(G["QP"][:, c, :], M.PJ[c % 2][:, :]).then_inc(s.sem("qp"), 1)
                act.wait_ge(s.sem("arg"), after(b, 2, 2))
                nc.scalar.activation(G["gv"][:, 4:6], G["gv"][:, 2:4], ACT.Exp, scale=-1.0).then_inc(s.sem("ge"), 1)
                def exponential(qb):
                    act.wait_ge(s.sem("sub"), after(b, 2 * TB, 2 * qb + 2))
                    nc.scalar.activation(G["S"][:, qb % 2, :, :], G["S"][:, qb % 2, :, :], ACT.Exp,
                                         scale=float(s.prm["dh"]) ** -0.5).then_inc(s.sem("e"), 1)

                exponential(0)
                for qb in range(TB):
                    act.wait_ge(s.sem("pt_ps"), after(b, TB, qb + 1))
                    nc.scalar.copy(G["PT"][:, 0:4, :], M.PJ[0][:, :].rearrange("p (c n) -> p c n", c=4)).then_inc(s.sem("pt"), 1)
                    nc.scalar.copy(G["PT"][:, 4, :], M.PJ[1][:, 0:P]).then_inc(s.sem("pt"), 1)
                    if qb + 1 < TB:
                        exponential(qb + 1)
                    act.wait_ge(s.sem("o_ps"), after(b, TB, qb + 1))
                    nc.scalar.copy(v["On"][:, qb, :], M.OB[:, 0:D]).then_inc(s.sem("on"), 1)
                out_act(act, s, b)

        def gated_dve(dve, s):
            v = V[s.name]
            start(dve, s, s.first)
            z = s.sem("zero")
            nc.vector.memset(G["Kbd"][:, :, :], 0.0).then_inc(z, 1)
            nc.vector.memset(G["Vbd"][:, :, :], 0.0).then_inc(z, 1)
            nc.vector.memset(G["ctD"][:, :, :], 0.0).then_inc(z, 1)
            nc.vector.memset(G["ctA"][:, :, :], 0.0).then_inc(z, 1)
            nc.vector.memset(G["wgb"][:, :, :], 1.0).then_inc(z, 1)
            dve.wait_ge(z, 5)
            dve.wait_ge(s.w_in, 16 * s.n_loads)
            for e, (_, w) in enumerate(CCH):
                nc.vector.tensor_scalar(G["wgb"][0:w, e, :], G["wgb"][0:w, e, :], G["wg"][0:w, e:e + 1], None, ALU.mult)
            gv, sc, ch = G["gv"], G["sc"], s.sem("chain")
            with dve.Fori(s.first, s.first + B) as b:
                start(dve, s, b)
                dve.wait_ge(s.sem("in_evac" + s.tag), after(b - s.first, 5, 5))
                for e, (_, w) in enumerate(CCH):
                    for name, at in (("ctD", 0), ("ctA", NTOK)):
                        dst = G[name][0:w, e, :].rearrange("p (r k) -> p r k", r=4)[:, :, at:at + NTOK]
                        nc.vector.tensor_copy(dst, M.cT[0:w, e, at:at + NTOK].unsqueeze(1).broadcast_to([w, 4, NTOK])).then_inc(s.sem("tok"), 1)
                dve.wait_ge(s.sem("k_ps"), after(b, 1, 1))
                for g in range(4):
                    q = slice(32 * g, 32 * g + 32)
                    nc.vector.tensor_copy(G["Kbd"][q, :, q], M.SM[0][q, 0:160].rearrange("p (c k) -> p c k", c=5)).then_inc(s.sem("kbd"), 1)
                nc.vector.reduce_sum(gv[:, 0:1], M.SM[0][:, 256:256 + NTOK], AX.X).then_inc(ch, 1)
                dve.wait_ge(ch, after(b, 3 + 3 * TB, 1))
                nc.vector.tensor_scalar(gv[:, 1:2], gv[:, 0:1], 1.0 / NTOK, sc[:, 0:1], ALU.mult, ALU.add).then_inc(ch, 1)
                dve.wait_ge(ch, after(b, 3 + 3 * TB, 2))
                nc.vector.tensor_tensor(gv[:, 2:3], sc[:, 2:3], gv[:, 1:2], ALU.add).then_inc(s.sem("arg"), 1)
                nc.vector.tensor_tensor(gv[:, 3:4], sc[:, 1:2], gv[:, 1:2], ALU.subtract).then_inc(s.sem("arg"), 1)
                dve.wait_ge(s.sem("v_ps"), after(b, 1, 1))
                for g in range(4):
                    q = slice(32 * g, 32 * g + 32)
                    nc.vector.tensor_copy(G["Vbd"][q, :, 16 * g:16 * g + 16],
                                          M.SM[1][q, 0:D].rearrange("p (c k) -> p c k", c=5)[:, :, 16 * g:16 * g + 16]).then_inc(s.sem("vbd"), 1)
                dve.wait_ge(s.sem("ge"), after(b, 1, 1))
                nc.vector.tensor_scalar(gv[:, 6:8], gv[:, 4:6], 1.0, None, ALU.add).then_inc(ch, 1)
                dve.wait_ge(ch, after(b, 3 + 3 * TB, 3))
                nc.vector.reciprocal(gv[:, 8:10], gv[:, 6:8]).then_inc(s.sem("gate"), 1)
                for qb in range(TB):
                    dve.wait_ge(s.sem("s_ps"), after(b, TB, qb + 1))
                    if qb >= 2:
                        dve.wait_ge(s.sem("pt_ps"), after(b, TB, qb - 1))
                    banks = ((M.ST[0][:, :], 0, 32), (M.ST[1][:, 0:P], 32, 8))
                    for src, g0, ng in banks:
                        last = nc.vector.reduce_max(G["mx"][:, g0:g0 + ng], src.rearrange("p (g k) -> p g k", k=NTOK), AX.X)
                        last.then_inc(s.sem("mx"), 1)
                    dve.wait_ge(s.sem("mx"), after(b, 2 * TB, 2 * qb + 2))
                    for src, g0, ng in banks:
                        nc.vector.tensor_tensor(G["S"][:, qb % 2, g0:g0 + ng, :], src.rearrange("p (g k) -> p g k", k=NTOK),
                                                G["mx"][:, g0:g0 + ng].unsqueeze(2).broadcast_to([P, ng, NTOK]), ALU.subtract).then_inc(s.sem("sub"), 1)
                    dve.wait_ge(s.sem("e"), after(b, TB, qb + 1))
                    nc.vector.reduce_sum(G["sum"][:, :], G["S"][:, qb % 2, :, :], AX.X).then_inc(ch, 1)
                    dve.wait_ge(ch, after(b, 3 + 3 * TB, 3 + 3 * qb + 1))
                    nc.vector.reciprocal(G["fac"][:, :], G["sum"][:, :]).then_inc(ch, 1)
                    dve.wait_ge(ch, after(b, 3 + 3 * TB, 3 + 3 * qb + 2))
                    dve.wait_ge(s.sem("gate"), after(b, 1, 1))
                    nc.vector.tensor_tensor(G["sum"][:, :].rearrange("p (h k) -> p h k", k=2), G["fac"][:, :].rearrange("p (h k) -> p h k", k=2),
                                            gv[:, 8:10].unsqueeze(1).broadcast_to([P, HEADS, 2]), ALU.mult).then_inc(ch, 1)
                    dve.wait_ge(ch, after(b, 3 + 3 * TB, 3 + 3 * qb + 3))
                    nc.vector.tensor_tensor(G["S"][:, qb % 2, :, :], G["S"][:, qb % 2, :, :], G["sum"][:, :].unsqueeze(2).broadcast_to([P, 40, NTOK]),
                                            ALU.mult).then_inc(s.sem("p"), 1)
                norm_next_dve(dve, s, b)
                out_dve(dve, s, b)

        def simple_sync(sp, s):
            load_weights(sp, s)
            if s.prm["cross"]:
                with sp.Fori(s.first, s.first + B) as b:
                    start(sp, s, b)
                    load_context(sp, s, b)

        block = ctx.enter_context(nc.Block())

        @block.sync
        def _(sp):
            sp.dma_start(M.x[:, :, :], io["x"].rearrange("(t p) d -> p t d", p=P)).then_inc(x_done, X_IN)
            for s in (wide, narrow):
                for what in SEEDED:
                    if what not in (("ox_ps",) if s is wide else ("q_ps", "k_ps", "q_evac", "k_evac", "psum", "den")):
                        sp.sem_inc(s.sem(what), 1)
            for s in stages:
                (attention_sync if s.kind == "att" else simple_sync)(sp, s)
            sp.wait_ge(x_done, X_IN + len(stages) * NX)
            sp.dma_start(io["out"].rearrange("(t p) d -> p t d", p=P), M.x[:, :, :]).then_inc(x_out, 16)
            sp.wait_ge(x_out, 16)

        @block.gpsimd
        def _(pool):
            nc.gpsimd.memset(M.mhalf[:, :], -0.5)
            nc.gpsimd.memset(M.ones[:, :], 1.0)
            nc.gpsimd.memset(M.ident[:, :], 0.0).then_inc(consts0, 1)
            nc.gpsimd.memset(M.nmT[:, :, :], 0.0).then_inc(consts0, 1)
            nc.gpsimd.memset(M.sel[:, :], 0.0).then_inc(consts0, 1)
            pool.wait_ge(consts0, 3)
            nc.gpsimd.affine_select(out=M.ident[:, :], in_=M.ident[:, :], compare_op=ALU.not_equal, fill=1.0, base=0,
                                    pattern=[[-1, P]], channel_multiplier=1).then_inc(consts, 1)
            pool.wait_ge(consts, 1)
            for k, row in enumerate((0, 32, 64 + 1, 96 + 1)):
                quadrant = slice(32 * (row // 32), 32 * (row // 32) + 32)
                nc.gpsimd.affine_select(out=M.sel[quadrant, :], in_=M.sel[quadrant, :], compare_op=ALU.not_equal, fill=1.0,
                                        base=-(row % 32), pattern=[[0, P]], channel_multiplier=1).then_inc(consts, 1)
                pool.wait_ge(consts, k + 2)
            norm_pool(pool, 0)
            for s in stages:
                if s.index * B == LN_BATCHES:
                    hold(pool, xn, TB * (LN_BATCHES + 1))
                    start(pool, s, s.first)
                    copy_pool(0)
                attention_pool(pool, s)

        @block.tensor
        def _(pe):
            pe.wait_ge(consts, 5)
            for s in stages:
                {"att": attention_pe, "ff": ff_pe, "gated": gated_pe}[s.kind](pe, s)

        @block.scalar
        def _(act):
            act.wait_ge(consts0, 3)
            for s in stages:
                {"att": attention_act, "ff": ff_act, "gated": gated_act}[s.kind](act, s)

        @block.vector
        def _(dve):
            dve.wait_ge(consts0, 3)
            for s in stages:
                if s.index == 0:
                    start(dve, s, 0)
                    norm_dve(dve, 0, 0)
                {"att": attention_dve, "ff": ff_dve, "gated": gated_dve}[s.kind](dve, s)


def kernel(**inputs):
    import numpy as np
    import concourse.bacc as bacc
    from concourse.bass_utils import run_bass_kernel_spmd

    nc = bacc.Bacc("TRN2", target_bir_lowering=False, num_devices=1)
    arrays = {}

    def arr(name):
        return np.asarray(inputs[name])

    def put(name, a):
        a = np.ascontiguousarray(a)
        arrays[name] = a
        return nc.dram_tensor(name, a.shape, mybir.dt.from_np(a.dtype), kind="ExternalInput").ap()

    def pairs(tag, wq, wk):
        nk = -(-wk.shape[0] // P)
        out = np.zeros((10, P, 3 + nk, P), wq.dtype)
        for w, off in ((wq, 0), (wk, 3)):
            for c in range(-(-w.shape[0] // P)):
                rows = w[c * P:(c + 1) * P]
                out[:, 0:rows.shape[0], off + c, :] = rows.reshape(rows.shape[0], 10, P).transpose(1, 0, 2)
        return put(tag, out.reshape(10 * P, (3 + nk) * P))

    def spread(tag, w):
        out = np.zeros((w.shape[0], HEADS, 32), w.dtype)
        out[:, :, 0:16] = w.reshape(w.shape[0], HEADS, 16)
        return put(tag, out.reshape(w.shape[0], HEADS * 32))

    def columns(a):
        out = np.zeros((-(-a.size // P), P), a.dtype)
        out.reshape(-1)[0:a.size] = a.reshape(-1)
        return out.T

    def by_dimension(w):
        return np.concatenate([w[:, a:a + n].reshape(-1, n // 16, 16).transpose(0, 2, 1).reshape(-1, n) for a, n in CH], 1)

    def plain(prefix, **names):
        order = {"g": columns, "be": columns, "b1": columns, "wq": by_dimension, "wk": by_dimension}
        return {k: put(f"in_{prefix}{v}", order.get(k, lambda a: a)(arr(prefix + v))) for k, v in names.items()}

    L0, L1, L2, L3 = "L0_xattn_", "L1_xattn_", "L2_xattn_", "L3_xattn_"
    io = {
        "x": put("in_x", arr("x").reshape(B * N, D)),
        "ctx": put("in_ctx", arr("ctx_768").reshape(B * N, CD)),
        "L0a": plain(L0, g="g1", be="be1", wv="wv1", wo="wo1", bo="bo1") | {"wqk": pairs("in_wqk1", arr(L0 + "wq1"), arr(L0 + "wk1"))},
        "L0b": plain(L0, g="g2", be="be2", wv="wv2", wo="wo2", bo="bo2") | {"wqk": pairs("in_wqk2", arr(L0 + "wq2"), arr(L0 + "wk2"))},
        "L0f": plain(L0, g="g3", be="be3", w1="w_ff1", b1="b_ff1", wo="w_ff2", bo="b_ff2"),
        "L1a": plain(L1, g="n1_g", be="n1_b", wq="q1", wk="k1", wv="v1", wo="o1_w", bo="o1_b"),
        "L1b": plain(L1, g="n2_g", be="n2_b", wq="q2", wk="k2", wv="v2", wo="o2_w", bo="o2_b"),
        "L1f": plain(L1, g="n3_g", be="n3_b", w1="ff_w1", b1="ff_b1", wo="ff_w2", bo="ff_b2"),
        "L2": {
            "wq": spread("in_l2q", arr(L2 + "w_q").T), "wk": spread("in_l2k", arr(L2 + "w_k").T),
            "wkd": spread("in_l2kd", arr(L2 + "w_k_dis").T),
            "wv": put("in_l2v", arr(L2 + "w_v").T), "wvd": put("in_l2vd", arr(L2 + "w_v_dis").T),
            "wo": put("in_l2o", arr(L2 + "w_out").T), "bo": put("in_l2bo", arr(L2 + "b_out")),
            "wg": put("in_l2g", columns(arr(L2 + "w_gate"))), "bg": put("in_l2bg", arr(L2 + "b_gate").reshape(1)),
            "al": put("in_l2al", arr(L2 + "anat_gate_logit").reshape(1)), "dl": put("in_l2dl", arr(L2 + "dis_gate_logit").reshape(1)),
        },
        "L3": plain(L3, wq="Wq", wk="Wk", wv="Wv", wo="Wo", bo="bo"),
        "out": nc.dram_tensor("out_0", (B * N, D), F32, kind="ExternalOutput").ap(),
    }
    program(nc, io)
    result = run_bass_kernel_spmd(nc, [arrays], core_ids=[0])
    return result.results[0]["out_0"].reshape(B, N, D)
```
